# Optimizing a Trainium2 kernel written in Bass

```python
import numpy as np
import jax
import jax.numpy as jnp

def _softmax(x, axis=-1):
    return jax.nn.softmax(x, axis=axis)

def _gelu(x):
    return jax.nn.gelu(x, approximate=True)

def _silu(x):
    return jax.nn.silu(x)

def _sigmoid(x):
    return jax.nn.sigmoid(x)

def _layernorm(x, axis=-1, eps=1e-05):
    m = jnp.mean(x, axis=axis, keepdims=True)
    v = jnp.var(x, axis=axis, keepdims=True)
    return (x - m) / jnp.sqrt(v + eps)

def _scatter_add(tgt, idx, src, axis=0):
    return tgt.at[idx].add(src)

def _segment_sum(src, seg, n):
    return jax.ops.segment_sum(src, seg, n)
kernel_name = 'mk_seq_preln_d1_jaxref_r4_45c061'

def setup_inputs(seed: int=0):
    np.random.seed(seed)
    _w = jnp.asarray

    def _L0_attn_setup():
        import jax, jax.numpy as jnp
        import numpy as np
        EMBED = 512
        HEADS = 16
        HEAD_DIM = EMBED // HEADS
        CHUNK = 128
        BASE = 10000.0
        EPS = 1e-06

        def _alibi_log_decay(h):
            slopes = 2.0 ** (-8.0 * (jnp.arange(h, dtype=jnp.float32) + 1.0) / h)
            return -slopes

        def _lrpe_rotate(x):
            b, n, h, d = x.shape
            half = d // 2
            theta = BASE ** (-2.0 * jnp.arange(half, dtype=jnp.float32) / d)
            ang = jnp.arange(n, dtype=jnp.float32)[:, None] * theta[None, :]
            cos = jnp.cos(ang)[None, :, None, :]
            sin = jnp.sin(ang)[None, :, None, :]
            x1, x2 = (x[..., :half], x[..., half:])
            return jnp.concatenate([x1 * cos - x2 * sin, x1 * sin + x2 * cos], axis=-1)

        def _lightning_attn(q, k, v, log_lam):
            b, n, h, d = q.shape
            C = CHUNK
            nc = n // C
            qc = q.reshape(b, nc, C, h, d).transpose(1, 0, 2, 3, 4)
            kc = k.reshape(b, nc, C, h, d).transpose(1, 0, 2, 3, 4)
            vc = v.reshape(b, nc, C, h, d).transpose(1, 0, 2, 3, 4)
            i = jnp.arange(C, dtype=jnp.float32)
            diff = i[:, None] - i[None, :]
            D = jnp.where(diff[None] >= 0, jnp.exp(log_lam[:, None, None] * diff[None]), 0.0)
            decay_q = jnp.exp(log_lam[None, :] * (i[:, None] + 1.0))
            decay_k = jnp.exp(log_lam[None, :] * (C - 1.0 - i[:, None]))
            lam_C = jnp.exp(log_lam * C)

            def step(S, qkv):
                qi, ki, vi = qkv
                scores = jnp.einsum('bthd,bshd->bhts', qi, ki) * D[None]
                o_intra = jnp.einsum('bhts,bshd->bthd', scores, vi)
                o_inter = jnp.einsum('bthd,bhde->bthe', qi * decay_q[None, :, :, None], S)
                S_new = lam_C[None, :, None, None] * S + jnp.einsum('bshd,bshe->bhde', ki * decay_k[None, :, :, None], vi)
                return (S_new, o_intra + o_inter)
            S0 = jnp.zeros((b, h, d, d), q.dtype)
            _, o = jax.lax.scan(step, S0, (qc, kc, vc))
            return o.transpose(1, 0, 2, 3, 4).reshape(b, n, h, d)

        def _gated_group_rmsnorm(o, gate, weight):
            b, n, d = o.shape
            x = o * jax.nn.sigmoid(gate)
            xg = x.reshape(b, n, HEADS, HEAD_DIM)
            ms = jnp.mean(xg * xg, axis=-1, keepdims=True)
            xg = xg * jax.lax.rsqrt(ms + EPS)
            return xg.reshape(b, n, d) * weight
        key = jax.random.key(seed)
        ks = jax.random.split(key, 8)
        b, n, d = (2, 512, EMBED)
        std = 0.02
        return {'x': jax.random.normal(ks[0], (b, n, d), jnp.float32), 'Wq': jax.random.normal(ks[1], (d, d), jnp.float32) * std, 'Wk': jax.random.normal(ks[2], (d, d), jnp.float32) * std, 'Wv': jax.random.normal(ks[3], (d, d), jnp.float32) * std, 'Wo': jax.random.normal(ks[4], (d, d), jnp.float32) * std, 'Wg1': jax.random.normal(ks[5], (d, HEAD_DIM), jnp.float32) * std, 'Wg2': jax.random.normal(ks[6], (HEAD_DIM, d), jnp.float32) * std, 'norm_weight': jnp.ones((d,), jnp.float32)}
    _L0_attn_in = _L0_attn_setup()

    def _L0_ffn_setup():
        import jax, jax.numpy as jnp
        import numpy as np
        BLOCK_SIZE = 32
        HIDDEN_SIZE = 512
        MLP_DIM = 4096
        NVFP4_LUT = jnp.array([0.0, 0.5, 1.0, 1.5, 2.0, 3.0, 4.0, 6.0, 0.0, -0.5, -1.0, -1.5, -2.0, -3.0, -4.0, -6.0], dtype=jnp.float32)

        def dequant_nvfp4(W_packed, scales, block=BLOCK_SIZE):
            N = W_packed.shape[0]
            low = W_packed & 15
            high = W_packed >> 4 & 15
            idx = jnp.stack([low, high], axis=-1).reshape(N, -1)
            vals = NVFP4_LUT[idx]
            K = vals.shape[1]
            vals = vals.reshape(N, K // block, block) * scales[:, :, None]
            return vals.reshape(N, K)
        key = jax.random.key(seed)
        ks = jax.random.split(key, 7)
        x = jax.random.normal(ks[0], (4, 32, HIDDEN_SIZE), dtype=jnp.float32)
        gate_W_packed = jax.random.randint(ks[1], (MLP_DIM, HIDDEN_SIZE // 2), 0, 64, dtype=jnp.int32)
        gate_scales = jax.random.uniform(ks[2], (MLP_DIM, HIDDEN_SIZE // BLOCK_SIZE), dtype=jnp.float32) * 0.1 + 0.001
        up_W_packed = jax.random.randint(ks[3], (MLP_DIM, HIDDEN_SIZE // 2), 0, 64, dtype=jnp.int32)
        up_scales = jax.random.uniform(ks[4], (MLP_DIM, HIDDEN_SIZE // BLOCK_SIZE), dtype=jnp.float32) * 0.1 + 0.001
        down_W_packed = jax.random.randint(ks[5], (HIDDEN_SIZE, MLP_DIM // 2), 0, 64, dtype=jnp.int32)
        down_scales = jax.random.uniform(ks[6], (HIDDEN_SIZE, MLP_DIM // BLOCK_SIZE), dtype=jnp.float32) * 0.1 + 0.001
        return {'x': x, 'gate_W_packed': gate_W_packed, 'gate_scales': gate_scales, 'up_W_packed': up_W_packed, 'up_scales': up_scales, 'down_W_packed': down_W_packed, 'down_scales': down_scales}
    _L0_ffn_in = _L0_ffn_setup()
    _d = {'L0_attn_x': _L0_attn_in['x'], 'L0_attn_Wq': _L0_attn_in['Wq'], 'L0_attn_Wk': _L0_attn_in['Wk'], 'L0_attn_Wv': _L0_attn_in['Wv'], 'L0_attn_Wo': _L0_attn_in['Wo'], 'L0_attn_Wg1': _L0_attn_in['Wg1'], 'L0_attn_Wg2': _L0_attn_in['Wg2'], 'L0_attn_norm_weight': _L0_attn_in['norm_weight'], 'L0_ffn_gate_W_packed': _L0_ffn_in['gate_W_packed'], 'L0_ffn_gate_scales': _L0_ffn_in['gate_scales'], 'L0_ffn_up_W_packed': _L0_ffn_in['up_W_packed'], 'L0_ffn_up_scales': _L0_ffn_in['up_scales'], 'L0_ffn_down_W_packed': _L0_ffn_in['down_W_packed'], 'L0_ffn_down_scales': _L0_ffn_in['down_scales']}
    _x0 = _d['L0_attn_x']
    _d['L0_attn_x'] = jax.random.normal(jax.random.fold_in(jax.random.key(seed), 1), (4, 512, 512), dtype=_x0.dtype)
    del _x0
    return _d

def reference(L0_attn_x, L0_attn_Wq, L0_attn_Wk, L0_attn_Wv, L0_attn_Wo, L0_attn_Wg1, L0_attn_Wg2, L0_attn_norm_weight, L0_ffn_gate_W_packed, L0_ffn_gate_scales, L0_ffn_up_W_packed, L0_ffn_up_scales, L0_ffn_down_W_packed, L0_ffn_down_scales):

    def _L0_attn_ref(x, Wq, Wk, Wv, Wo, Wg1, Wg2, norm_weight):
        import jax, jax.numpy as jnp
        import numpy as np
        EMBED = 512
        HEADS = 16
        HEAD_DIM = EMBED // HEADS
        CHUNK = 128
        BASE = 10000.0
        EPS = 1e-06

        def _alibi_log_decay(h):
            slopes = 2.0 ** (-8.0 * (jnp.arange(h, dtype=jnp.float32) + 1.0) / h)
            return -slopes

        def _lrpe_rotate(x):
            b, n, h, d = x.shape
            half = d // 2
            theta = BASE ** (-2.0 * jnp.arange(half, dtype=jnp.float32) / d)
            ang = jnp.arange(n, dtype=jnp.float32)[:, None] * theta[None, :]
            cos = jnp.cos(ang)[None, :, None, :]
            sin = jnp.sin(ang)[None, :, None, :]
            x1, x2 = (x[..., :half], x[..., half:])
            return jnp.concatenate([x1 * cos - x2 * sin, x1 * sin + x2 * cos], axis=-1)

        def _lightning_attn(q, k, v, log_lam):
            b, n, h, d = q.shape
            C = CHUNK
            nc = n // C
            qc = q.reshape(b, nc, C, h, d).transpose(1, 0, 2, 3, 4)
            kc = k.reshape(b, nc, C, h, d).transpose(1, 0, 2, 3, 4)
            vc = v.reshape(b, nc, C, h, d).transpose(1, 0, 2, 3, 4)
            i = jnp.arange(C, dtype=jnp.float32)
            diff = i[:, None] - i[None, :]
            D = jnp.where(diff[None] >= 0, jnp.exp(log_lam[:, None, None] * diff[None]), 0.0)
            decay_q = jnp.exp(log_lam[None, :] * (i[:, None] + 1.0))
            decay_k = jnp.exp(log_lam[None, :] * (C - 1.0 - i[:, None]))
            lam_C = jnp.exp(log_lam * C)

            def step(S, qkv):
                qi, ki, vi = qkv
                scores = jnp.einsum('bthd,bshd->bhts', qi, ki) * D[None]
                o_intra = jnp.einsum('bhts,bshd->bthd', scores, vi)
                o_inter = jnp.einsum('bthd,bhde->bthe', qi * decay_q[None, :, :, None], S)
                S_new = lam_C[None, :, None, None] * S + jnp.einsum('bshd,bshe->bhde', ki * decay_k[None, :, :, None], vi)
                return (S_new, o_intra + o_inter)
            S0 = jnp.zeros((b, h, d, d), q.dtype)
            _, o = jax.lax.scan(step, S0, (qc, kc, vc))
            return o.transpose(1, 0, 2, 3, 4).reshape(b, n, h, d)

        def _gated_group_rmsnorm(o, gate, weight):
            b, n, d = o.shape
            x = o * jax.nn.sigmoid(gate)
            xg = x.reshape(b, n, HEADS, HEAD_DIM)
            ms = jnp.mean(xg * xg, axis=-1, keepdims=True)
            xg = xg * jax.lax.rsqrt(ms + EPS)
            return xg.reshape(b, n, d) * weight
        b, n, d = x.shape
        q = (x @ Wq).reshape(b, n, HEADS, HEAD_DIM)
        k = (x @ Wk).reshape(b, n, HEADS, HEAD_DIM)
        v = (x @ Wv).reshape(b, n, HEADS, HEAD_DIM)
        q = jax.nn.silu(q)
        k = jax.nn.silu(k)
        q = _lrpe_rotate(q)
        k = _lrpe_rotate(k)
        log_lam = _alibi_log_decay(HEADS)
        o = _lightning_attn(q, k, v, log_lam).reshape(b, n, d)
        gate = x @ Wg1 @ Wg2
        o = _gated_group_rmsnorm(o, gate, norm_weight)
        return o @ Wo

    def _L0_ffn_ref(x, gate_W_packed, gate_scales, up_W_packed, up_scales, down_W_packed, down_scales):
        import jax, jax.numpy as jnp
        import numpy as np
        BLOCK_SIZE = 32
        HIDDEN_SIZE = 512
        MLP_DIM = 4096
        NVFP4_LUT = jnp.array([0.0, 0.5, 1.0, 1.5, 2.0, 3.0, 4.0, 6.0, 0.0, -0.5, -1.0, -1.5, -2.0, -3.0, -4.0, -6.0], dtype=jnp.float32)

        def dequant_nvfp4(W_packed, scales, block=BLOCK_SIZE):
            N = W_packed.shape[0]
            low = W_packed & 15
            high = W_packed >> 4 & 15
            idx = jnp.stack([low, high], axis=-1).reshape(N, -1)
            vals = NVFP4_LUT[idx]
            K = vals.shape[1]
            vals = vals.reshape(N, K // block, block) * scales[:, :, None]
            return vals.reshape(N, K)
        B, S, H = x.shape
        xt = x.reshape(B * S, H)
        Wg = dequant_nvfp4(gate_W_packed, gate_scales)
        Wu = dequant_nvfp4(up_W_packed, up_scales)
        Wd = dequant_nvfp4(down_W_packed, down_scales)
        gate = jnp.einsum('th,nh->tn', xt, Wg)
        up = jnp.einsum('th,nh->tn', xt, Wu)
        gelu = jnp.tanh(0.7978845608028654 * (gate + 0.044715 * gate ** 3)) * gate * 0.5 + gate * 0.5
        inter = gelu * up
        out = jnp.einsum('tn,hn->th', inter, Wd)
        return out.reshape(B, S, H)
    x = L0_attn_x
    x = x + _L0_attn_ref(_layernorm(x, axis=-1), L0_attn_Wq, L0_attn_Wk, L0_attn_Wv, L0_attn_Wo, L0_attn_Wg1, L0_attn_Wg2, L0_attn_norm_weight)
    x = x + _L0_ffn_ref(_layernorm(x, axis=-1), L0_ffn_gate_W_packed, L0_ffn_gate_scales, L0_ffn_up_W_packed, L0_ffn_up_scales, L0_ffn_down_W_packed, L0_ffn_down_scales)
    return x

_drawn_inputs = setup_inputs


def setup_inputs(seed=0):
    import zlib

    import numpy as np

    out = dict(_drawn_inputs(seed))
    spreads = {'L0_attn_norm_weight': (1.0, 0.2)}
    factors = {'L0_attn_Wg1': 4.331, 'L0_attn_Wg2': 4.271}
    for name, (base, spread) in spreads.items():
        noise = np.random.default_rng([zlib.crc32(name.encode()), seed]).standard_normal(out[name].shape)
        drawn = base * np.exp(spread * noise) if base else spread * noise
        out[name] = jnp.asarray(drawn.astype(out[name].dtype))
    for name, factor in factors.items():
        out[name] = (out[name] * factor).astype(out[name].dtype)
    return out
```

```python
from contextlib import ExitStack

import numpy as np

import concourse.bass as bass
from concourse import mybir
from concourse.alu_op_type import AluOpType as ALU

ACT = mybir.ActivationFunctionType
F32 = mybir.dt.float32
F32R = mybir.dt.float32r
F16 = mybir.dt.float16
I32 = mybir.dt.int32

P = 128
BATCH, SEQ, EMBED = 4, 512, 512
HEADS, HD = 16, 32
MLP = 4096
KT = EMBED // P
CHUNKS = SEQ // P
TILES = BATCH * CHUNKS
QB = 4
BLK = 256
BLOCKS = MLP // BLK
UNITS = 3
TB = 512
TBS = TILES * P // TB
LN_EPS, RMS_EPS = 1e-5, 1e-6
GELU_C, GELU_A = 0.7978845608028654, 0.044715
RSQRT_SEED = 1597463007.0
GATE, UP, DOWN = range(UNITS)


def shape_constants():
    f = np.float32
    half = HD // 2
    theta = np.power(f(10000.0), f(-2.0) * np.arange(half, dtype=f) / f(HD)).astype(f)
    ang = np.arange(SEQ, dtype=f)[:, None] * theta[None, :]
    cos, sin = np.cos(ang.astype(np.float64)), np.sin(ang.astype(np.float64))
    rot = np.stack([np.concatenate([cos, cos], 1), np.concatenate([-sin, sin], 1)], 0) * 0.5
    rot = rot.reshape(2, CHUNKS, P, HD).transpose(2, 0, 1, 3).astype(f)
    lam = -(2.0 ** (-8.0 * (np.arange(HEADS) + 1.0) / HEADS)).astype(f).astype(np.float64)
    i = np.arange(P)
    diff = (i[None, :] - i[:, None]).astype(np.float64)
    mask = np.where(diff[None] >= 0, np.exp(lam[:, None, None] * np.maximum(diff[None], 0)), 0.0)
    mask = mask.reshape(KT, QB, P, P).transpose(2, 1, 0, 3).astype(f)
    decay_q = np.exp(lam[:, None] * (i[None, :] + 1.0)).reshape(KT, QB, P)
    decay_q = np.repeat(decay_q.transpose(1, 0, 2), HD, axis=0).astype(f)
    decay_k = np.exp(lam[None, :] * (P - 1.0 - i[:, None])).astype(f)
    lam_c = np.repeat(np.exp(lam * P).reshape(KT, QB).T, HD, axis=0).astype(f)
    c = np.ascontiguousarray
    return {"rot": c(rot), "mask": c(mask), "decay_q": c(decay_q), "decay_k": c(decay_k),
            "lam_c": c(lam_c), "ident": np.eye(P, dtype=f)}


def build(nc, x, wq, wk, wv, wo, wg1, wg2, norm_w, packed, scales,
          rot, mask, decay_q, decay_k, lam_c, ident, out):
    ctx = ExitStack()
    with ctx:
        def sb(name, shape, dt=F32, scope=ctx):
            return scope.enter_context(nc.sbuf_tensor(name, shape, dt))

        def sem(name):
            return ctx.enter_context(nc.semaphore(name))

        acc = sb("acc", [P, TILES, EMBED])
        idt = sb("idt", [P, P])
        pk = sb("pk", [P, UNITS, 512], I32)
        sc = sb("sc", [P, UNITS, 512])
        nib = sb("nib", [P, 512], I32)
        wf = sb("wf", [P, 2, 512])
        ln1 = sb("ln1", [P, TILES, 2])
        ln2 = sb("ln2", [P, TILES, 2])
        r1 = sb("r1", [P, TILES])
        nm1 = sb("nm1", [P, TILES])
        r2 = sb("r2", [P, TILES])
        nt_v = sb("nt_v", [P, 16])
        nt_t = sb("nt_t", [P, 16])
        bst = sb("bst", [P, 6])
        bst1 = sb("bst1", [P, TILES, 6])
        with ExitStack() as early:
            w_in = sb("w_in", [P, 3, KT * 512], F32, early)
        wh0 = sb("wh0", [P, UNITS, 1024], F32R)
        wl0 = sb("wl0", [P, UNITS, 1024], F32R)
        with ExitStack() as att_w:
            w_hi = [sb(f"w_hi{n}", [P, KT, 512], F32R, att_w) for n in range(4)]
            w_lo = [sb(f"w_lo{n}", [P, KT, 512], F32R, att_w) for n in range(4)]
        x1h = sb("x1h", [P, KT, TILES * P], F32R)
        x1l = sb("x1l", [P, KT, TILES * P], F32R)
        with ExitStack() as att:
            g1h = sb("g1h", [P, KT, P], F32R, att)
            g1l = sb("g1l", [P, KT, P], F32R, att)
            g2s = sb("g2s", [P, 512], F32R, att)
            nw = sb("nw", [P, KT], F32, att)
            rotT = sb("rotT", [P, 2, CHUNKS, HD], F32, att)
            maskT = sb("maskT", [P, QB, 512], F32, att)
            dqT = sb("dqT", [P, KT, P], F32, att)
            dkT = sb("dkT", [P, HEADS], F32, att)
            lamT = sb("lamT", [P, KT], F32, att)
            xn = sb("xn", [P, 512], F32, att)
            xth = sb("xth", [P, KT, P], F32R, att)
            xtl = sb("xtl", [P, KT, P], F32R, att)
            qa = sb("qa", [P, 2, 512], F32, att)
            rb = sb("rb", [P, 2, 512], F32, att)
            qr = sb("qr", [P, 2, 512], F32, att)
            g1_in = rb[:, 1, 0:KT * HD].rearrange("p (k d) -> p k d", k=KT)
            g2_in = rb[:, 0, :]
            kd = sb("kd", [P, 512], F32, att)
            qT = sb("qT", [P, KT, P], F32, att)
            kT = sb("kT", [P, KT, P], F32, att)
            qdT = sb("qdT", [P, KT, P], F32, att)
            g4 = sb("g4", [P, P], F32R, att)
            g4h = sb("g4h", [P, P], F32R, att)
            vs = sb("vs", [P, 2, 512], F32, att)
            tg = sb("tg", [P, 512], F32, att)
            pr = sb("pr", [P, QB, 512], F32, att)
            st = sb("st", [P, KT, P], F32, att)
            xg = sb("xg", [P, 512], F32, att)
            sq = sb("sq", [P, 512], F32, att)
            oth = sb("oth", [P, KT, P], F32R, att)
            otl = sb("otl", [P, KT, P], F32R, att)
            ms = sb("ms", [P, HEADS], F32, att)
            rr = sb("rr", [P, HEADS], F32, att)
        wh1 = sb("wh1", [P, UNITS, 1024], F32R)
        wl1 = sb("wl1", [P, UNITS, 1024], F32R)
        hx = [sb(f"hx{n}", [P, 512]) for n in range(2)]
        hh = [sb(f"hh{n}", [P, 512], F32R) for n in range(2)]
        hl = [sb(f"hl{n}", [P, 512], F32R) for n in range(2)]
        wh, wl = [wh0, wh1], [wl0, wl1]

        bank = [ctx.enter_context(nc.psum_tensor(f"bank{n}", [P, 512], F32)) for n in range(8)]
        BQ, BK, BS, BV, BO = bank[0], bank[1], bank[2:6], bank[6], bank[7]
        BG, BU, BY = bank[0:4:2], bank[1:4:2], bank[4:8]
        BX = bank[6:8]

        s_x = [sem(f"s_x{b}") for b in range(BATCH)]
        s_nw = sem("s_nw")
        s_id = sem("s_id")
        s_w = [sem(f"s_w{n}") for n in range(4)]
        s_small = sem("s_small")
        s_tab = sem("s_tab")
        s_unit = [sem(f"s_unit{u}") for u in range(UNITS)]
        s_out = sem("s_out")
        s_whi = sem("s_whi")
        s_wlo = sem("s_wlo")
        s_wob = sem("s_wob")
        s_ghi = sem("s_ghi")
        s_glo = sem("s_glo")
        s_bn1 = sem("s_bn1")
        s_ln1 = sem("s_ln1")
        s_nt = sem("s_nt")
        s_ntl = sem("s_ntl")
        s_r1 = sem("s_r1")
        s_vlo = sem("s_vlo")
        s_st0 = sem("s_st0")
        xn_done = sem("xn_done")
        xt_ps, xt_hi, xt_lo = sem("xt_ps"), sem("xt_hi"), sem("xt_lo")
        qk_ps, g1_ps, v_ps, gate_ps = sem("qk_ps"), sem("g1_ps"), sem("v_ps"), sem("gate_ps")
        g_hi, g_lo = sem("g_hi"), sem("g_lo")
        qk_tanh, qk_silu = sem("qk_tanh"), sem("qk_silu")
        v_sb, gate_tanh = sem("v_sb"), sem("gate_tanh")
        rope_a, rope_b, rope_c = sem("rope_a"), sem("rope_b"), sem("rope_c")
        kd_done = sem("kd_done")
        qkt_ps, qt_sb, kt_sb, qd_sb = sem("qkt_ps"), sem("qt_sb"), sem("kt_sb"), sem("qd_sb")
        score_ps, prob_sb = sem("score_ps"), sem("prob_sb")
        inter_ps, o_ps, kv_ps = sem("inter_ps"), sem("o_ps"), sem("kv_ps")
        st_scaled, st_done = sem("st_scaled"), sem("st_done")
        xg_done, sq_done, ms_done, on_done = (sem("xg_done"), sem("sq_done"), sem("ms_done"),
                                              sem("on_done"))
        ot_ps, ot_hi, ot_lo, wo_ps = sem("ot_ps"), sem("ot_hi"), sem("ot_lo"), sem("wo_ps")
        x1_done, x1_row, bn_done = sem("x1_done"), sem("x1_row"), sem("bn_done")
        bst_done, ln2_done = sem("bst_done"), sem("ln2_done")
        dq_bits, dq_f, dq_hi, dq_lo = sem("dq_bits"), sem("dq_f"), sem("dq_hi"), sem("dq_lo")
        n2_done = sem("n2_done")
        x1t_ps, x1t_hi, x1t_lo = sem("x1t_ps"), sem("x1t_hi"), sem("x1t_lo")
        g_ps = [sem(f"g_ps{n}") for n in range(2)]
        u_ps = [sem(f"u_ps{n}") for n in range(2)]
        h_sq = [sem(f"h_sq{n}") for n in range(2)]
        h_arg = [sem(f"h_arg{n}") for n in range(2)]
        h_tanh = [sem(f"h_tanh{n}") for n in range(2)]
        h_gelu = [sem(f"h_gelu{n}") for n in range(2)]
        h_prod = [sem(f"h_prod{n}") for n in range(2)]
        h_hi = [sem(f"h_hi{n}") for n in range(2)]
        h_lo = [sem(f"h_lo{n}") for n in range(2)]
        y_ps = [sem(f"y_ps{n}") for n in range(2)]
        y_add = sem("y_add")

        NT = 11

        def batches(eng, body):
            for c in range(CHUNKS):
                body(0, c)
            with eng.Fori(1, BATCH - 1) as b:
                for c in range(CHUNKS):
                    body(b, c)
            for c in range(CHUNKS):
                body(BATCH - 1, c)

        def near_end(b, c, ahead):
            return isinstance(b, int) and b * CHUNKS + c + ahead >= TILES

        def at_start(b, c):
            return isinstance(b, int) and b == 0 and c == 0

        def kvs(b, c):
            return b * (CHUNKS - 1) + c

        block = ctx.enter_context(nc.Block())

        @block.sync
        def _(sp):
            xv = x.rearrange("b (c p) d -> p (b c) d", p=P)
            w_view = [w.rearrange("(k p) n -> p k n", p=P) for w in (wq, wk, wv, wo)]

            def load_x(b):
                sp.dma_start(acc[:, 4 * b:4 * b + 4, :], xv[:, 4 * b:4 * b + 4, :]
                             ).then_inc(s_x[b], 16)

            def load_w(n, slot):
                sp.dma_start(w_in[:, slot, :].rearrange("p (k n) -> p k n", k=KT),
                             w_view[n]).then_inc(s_w[n], 16)

            load_x(0)
            sp.dma_start(idt[:], ident).then_inc(s_id, 16)
            load_w(0, 0)
            load_w(1, 1)
            sp.dma_start(g1_in, wg1.rearrange("(k p) n -> p k n", p=P)).then_inc(s_small, 16)
            for r in range(4):
                sp.dma_start(g2_in[32 * r:32 * r + 32, :], wg2).then_inc(s_small, 16)
            load_w(2, 2)
            sp.dma_start(rotT[:], rot).then_inc(s_tab, 16)
            sp.dma_start(maskT[:], mask.rearrange("p r g t -> p r (g t)")).then_inc(s_tab, 16)
            sp.dma_start(dqT[:], decay_q).then_inc(s_tab, 16)
            sp.dma_start(dkT[:], decay_k).then_inc(s_tab, 16)
            sp.dma_start(lamT[:], lam_c).then_inc(s_tab, 16)
            for b in range(1, BATCH):
                load_x(b)
            sp.dma_start(nw[:], norm_w).then_inc(s_nw, 16)
            sp.wait_ge(s_whi, 1)
            sp.wait_ge(s_wlo, 1)
            load_w(3, 0)

            def load_unit(q, u):
                sp.dma_start(pk[:, u, :], packed[bass.ds(q * UNITS + u, 1), :, :]
                             .rearrange("a p w -> p (a w)")).then_inc(s_unit[u], 16)
                src = scales[bass.ds(q * UNITS + u, 1), :, :].rearrange("a r w -> (a r) w")
                sp.dma_start(sc[:, u, :], src.unsqueeze(1).broadcast_to([8, 16, 512])
                             ).then_inc(s_unit[u], 16)

            for u in range(UNITS):
                load_unit(0, u)
            with sp.Fori(1, BLOCKS) as q:
                for u in range(UNITS):
                    sp.wait_ge(dq_f, q * UNITS - UNITS + u + 1)
                    load_unit(q, u)
            ov = out.rearrange("b (c p) d -> p (b c) d", p=P)
            for tb in range(TBS):
                sp.wait_ge(y_add, 4 * (TBS * (BLOCKS - 1) + tb + 1))
                sp.dma_start(ov[:, 4 * tb:4 * tb + 4, :], acc[:, 4 * tb:4 * tb + 4, :]
                             ).then_inc(s_out, 16)
            sp.wait_ge(s_out, 16 * TBS)

        @block.scalar
        def _(act):
            A = nc.scalar.activation

            def weight_hi(n, slot):
                act.wait_ge(s_w[n], 16)
                A(w_hi[n][:], w_in[:, slot, :].rearrange("p (k n) -> p k n", k=KT),
                  ACT.Copy).then_inc(s_whi, 1)

            def norm1(t, ln):
                act.wait_ge(s_r1, ln)
                act.wait_ge(xt_ps, t)
                A(xn[:], acc[:, bass.ds(t, 1), :].rearrange("p a d -> p (a d)"), ACT.Identity,
                  bias=nm1[:, bass.ds(t, 1)], scale=r1[:, bass.ds(t, 1)]).then_inc(xn_done, 1)

            def xt_hi_(t):
                act.wait_ge(xt_ps, t + 1)
                act.wait_ge(v_ps, t)
                A(xth[:], BV[:].rearrange("p (k t) -> p k t", k=KT), ACT.Copy).then_inc(xt_hi, 1)

            def gate_low(t):
                act.wait_ge(g1_ps, t + 1)
                act.wait_ge(gate_ps, t)
                A(g4h[64:128, :], BS[3][64:128, 0:P], ACT.Copy)
                A(g4[0:64, :], BS[3][0:64, 0:P], ACT.Copy).then_inc(g_hi, 1)

            def tanh_qk(t):
                act.wait_ge(qk_ps, t + 1)
                act.wait_ge(qk_silu, t)
                if not (isinstance(t, int) and t == 0):
                    act.wait_ge(rope_c, t)
                A(qa[:, 0, :], BQ[:], ACT.Tanh, scale=0.5)
                A(qa[:, 1, :], BK[:], ACT.Tanh, scale=0.5).then_inc(qk_tanh, 1)

            def v_copy(t, par):
                act.wait_ge(v_ps, t + 1)
                if not (isinstance(t, int) and t < 2):
                    act.wait_ge(o_ps, t - 1)
                A(vs[:, par, :], BV[:], ACT.Copy).then_inc(v_sb, 1)

            def tanh_gate(t):
                act.wait_ge(gate_ps, t + 1)
                act.wait_ge(xg_done, t)
                A(tg[:], BS[3][:], ACT.Tanh, scale=0.5).then_inc(gate_tanh, 1)

            def square(t):
                act.wait_ge(xg_done, t + 1)
                act.wait_ge(ot_ps, t)
                A(sq[:], xg[:], ACT.Square).then_inc(sq_done, 1)

            def ot_hi_(t):
                act.wait_ge(ot_ps, t + 1)
                act.wait_ge(wo_ps, t)
                A(oth[:], BS[2][:].rearrange("p (k t) -> p k t", k=KT), ACT.Copy).then_inc(ot_hi, 1)

            def unit_hi(k, u, par):
                act.wait_ge(dq_f, k + 1)
                A(wh[par][:, bass.ds(u, 1), :].rearrange("p a w -> p (a w)"),
                  wf[:].rearrange("p a w -> p (a w)"), ACT.Copy).then_inc(dq_hi, 1)

            weight_hi(0, 0)
            norm1(0, 1)
            weight_hi(1, 1)
            xt_hi_(0)
            norm1(1, 1)
            act.wait_ge(s_small, 16 * 5)
            A(g1h[:].rearrange("p k (r d) -> p k r d", r=4),
              g1_in.unsqueeze(2).broadcast_to([P, KT, 4, HD]), ACT.Copy).then_inc(s_ghi, 1)
            for r in range(4):
                A(g2s[32 * r:32 * r + 32, :], g2_in[32 * r:32 * r + 32, :],
                  ACT.Copy).then_inc(s_ghi, 1)
            weight_hi(2, 2)
            tanh_qk(0)
            gate_low(0)
            v_copy(0, 0)
            xt_hi_(1)
            norm1(2, 1)
            tanh_gate(0)
            act.wait_ge(s_wob, 1)
            A(w_hi[3][:], w_in[:, 0, :].rearrange("p (k n) -> p k n", k=KT),
              ACT.Copy).then_inc(s_whi, 1)

            def tile(b, c):
                t = CHUNKS * b + c
                act.wait_ge(qkt_ps, t + 1)
                act.wait_ge(score_ps, QB * t)
                A(qT[:], BS[0][:].rearrange("p (k t) -> p k t", k=KT), ACT.Copy).then_inc(qt_sb, 1)
                A(kT[:], BS[1][:].rearrange("p (k t) -> p k t", k=KT), ACT.Copy).then_inc(kt_sb, 1)
                if not at_start(b, c):
                    square(t - 1)
                if not near_end(b, c, 1):
                    tanh_qk(t + 1)
                    gate_low(t + 1)
                if not at_start(b, c):
                    ot_hi_(t - 1)
                if not near_end(b, c, 1):
                    v_copy(t + 1, (c + 1) % 2)
                if not near_end(b, c, 2):
                    xt_hi_(t + 2)
                if not near_end(b, c, 3):
                    ahead = (c + 3) // CHUNKS + 1
                    norm1(t + 3, b + ahead)
                if not near_end(b, c, 1):
                    tanh_gate(t + 1)
                if c == 2 and not near_end(b, c, 4):
                    unit_hi(b, b, 0)

            batches(act, tile)
            square(TILES - 1)
            ot_hi_(TILES - 1)

            with act.Fori(0, TILES // 2) as h:
                for par in range(2):
                    act.wait_ge(x1t_ps, 2 * h + par + 1)
                    A(x1h[:, :, bass.ds((2 * h + par) * P, P)],
                      BX[par][:].rearrange("p (k t) -> p k t", k=KT), ACT.Copy
                      ).then_inc(x1t_hi, 1)

            def step(q, par_q, tb):
                s = TBS * q + tb
                for par in range(2):
                    act.wait_ge(g_ps[par], s + 1)
                    act.wait_ge(h_lo[par], s)
                    A(hx[par][:], BG[par][:], ACT.Square).then_inc(h_sq[par], 1)
                    act.wait_ge(h_arg[par], s + 1)
                    A(hx[par][:], hx[par][:], ACT.Tanh, scale=GELU_C * GELU_A
                      ).then_inc(h_tanh[par], 1)
                    if par == 1 and tb >= 1 and not (isinstance(q, int) and q == BLOCKS - 1):
                        unit_hi(UNITS * (q + 1) + tb - 1, tb - 1, 1 - par_q)
                    act.wait_ge(h_prod[par], s + 1)
                    act.wait_ge(y_ps[par], s)
                    A(hh[par][:], hx[par][:], ACT.Copy).then_inc(h_hi[par], 1)

            pairs(act, step)

        @block.vector
        def _(dve):
            V = nc.vector

            def newton(steps, v, n, r, base, scale, eps):
                vv, tt = nt_v[:, 0:n], nt_t[:, 0:n]
                k = [0]

                def done(ins):
                    k[0] += 1
                    ins.then_inc(steps, 1)
                    dve.wait_ge(steps, base + k[0])

                done(V.tensor_scalar(vv, v, scale, eps, ALU.mult, ALU.add))
                done(V.tensor_scalar(r.bitcast(I32), vv.bitcast(I32), -0.5, RSQRT_SEED,
                                     ALU.mult, ALU.add))
                for _ in range(3):
                    done(V.scalar_tensor_tensor(out=tt, in0=r, scalar=-0.5, in1=r,
                                                op0=ALU.mult, op1=ALU.mult))
                    done(V.tensor_tensor(tt, tt, vv, ALU.mult))
                    done(V.scalar_tensor_tensor(out=r, in0=tt, scalar=1.5, in1=r,
                                                op0=ALU.add, op1=ALU.mult))
                assert k[0] == NT

            def stats(b):
                rows = slice(CHUNKS * b, CHUNKS * b + CHUNKS)
                dve.wait_ge(s_x[b], 16)
                for t in range(CHUNKS * b, CHUNKS * b + CHUNKS):
                    V.bn_stats(bst1[:, t, :], acc[:, t, :]).then_inc(s_bn1, 1)
                for t in range(CHUNKS * b, CHUNKS * b + CHUNKS):
                    dve.wait_ge(s_bn1, t + 1)
                    V.bn_aggr(ln1[:, t, :], bst1[:, t, :]).then_inc(s_ln1, 1)
                dve.wait_ge(s_ln1, CHUNKS * b + CHUNKS)
                newton(s_ntl, ln1[:, rows, 1], CHUNKS, r1[:, rows], NT * b, 1.0, LN_EPS)
                V.scalar_tensor_tensor(out=nm1[:, rows], in0=ln1[:, rows, 0], scalar=-1.0,
                                       in1=r1[:, rows], op0=ALU.mult, op1=ALU.mult
                                       ).then_inc(s_r1, 1)

            def weight_lo(n, slot, his):
                dve.wait_ge(s_whi, his)
                V.tensor_tensor(w_lo[n][:], w_in[:, slot, :].rearrange("p (k n) -> p k n", k=KT),
                                w_hi[n][:].bitcast(F32), ALU.subtract).then_inc(s_wlo, 1)

            def xt_lo_(t):
                dve.wait_ge(xt_hi, t + 1)
                V.tensor_tensor(xtl[:], BV[:].rearrange("p (k t) -> p k t", k=KT),
                                xth[:].bitcast(F32), ALU.subtract).then_inc(xt_lo, 1)

            def gate_low(t):
                dve.wait_ge(g_hi, t + 1)
                V.tensor_tensor(g4[64:128, :], BS[3][64:128, 0:P], g4h[64:128, :].bitcast(F32),
                                ALU.subtract).then_inc(g_lo, 1)

            def silu_qk(t):
                dve.wait_ge(qk_tanh, t + 1)
                V.scalar_tensor_tensor(out=qa[:, 0, :], in0=qa[:, 0, :], scalar=1.0, in1=BQ[:],
                                       op0=ALU.add, op1=ALU.mult)
                V.scalar_tensor_tensor(out=qa[:, 1, :], in0=qa[:, 1, :], scalar=1.0, in1=BK[:],
                                       op0=ALU.add, op1=ALU.mult).then_inc(qk_silu, 1)

            def gated(t):
                dve.wait_ge(o_ps, t + 1)
                dve.wait_ge(gate_tanh, t + 1)
                dve.wait_ge(on_done, t)
                V.scalar_tensor_tensor(out=xg[:], in0=tg[:], scalar=1.0, in1=BO[:],
                                       op0=ALU.add, op1=ALU.mult).then_inc(xg_done, 1)

            def normed(t):
                dve.wait_ge(sq_done, t + 1)
                V.tensor_reduce(ms[:], sq[:].rearrange("p (h d) -> p h d", d=HD),
                                mybir.AxisListType.X, ALU.add).then_inc(ms_done, 1)
                dve.wait_ge(ms_done, t + 1)
                newton(s_nt, ms[:], HEADS, rr[:], NT * t, 1.0 / HD, 4 * RMS_EPS)
                V.tensor_tensor(sq[:].rearrange("p (h d) -> p h d", d=HD),
                                xg[:].rearrange("p (h d) -> p h d", d=HD),
                                rr[:].unsqueeze(2).broadcast_to([P, HEADS, HD]),
                                ALU.mult).then_inc(on_done, 1)

            def ot_lo_(t):
                dve.wait_ge(ot_hi, t + 1)
                V.tensor_tensor(otl[:], BS[2][:].rearrange("p (k t) -> p k t", k=KT),
                                oth[:].bitcast(F32), ALU.subtract).then_inc(ot_lo, 1)

            def add_x1(t):
                dve.wait_ge(wo_ps, t + 1)
                row = acc[:, bass.ds(t, 1), :].rearrange("p a d -> p (a d)")
                V.tensor_tensor(sq[:], row, BQ[:], ALU.add).then_inc(x1_done, 1)
                dve.wait_ge(x1_done, t + 1)
                V.bn_stats(bst[:], sq[:]).then_inc(bn_done, 1)
                V.tensor_scalar(row, sq[:], 1.0, None, ALU.mult).then_inc(x1_row, 1)
                dve.wait_ge(bn_done, t + 1)
                V.tensor_scalar(bst1[:, bass.ds(t, 1), :].rearrange("p a d -> p (a d)"), bst[:],
                                1.0, None, ALU.mult).then_inc(bst_done, 1)

            def unit_bits(k, u, loads):
                w = pk[:, bass.ds(u, 1), :].rearrange("p a w -> p (a w)")
                for n, wait in enumerate(loads):
                    dve.wait_ge(s_unit[n], wait)
                k5 = 5 * k
                V.tensor_scalar(nib[:], w, 12, 0x000F0000, ALU.logical_shift_left,
                                ALU.bitwise_and).then_inc(dq_bits, 1)
                dve.wait_ge(dq_bits, k5 + 1)
                V.scalar_tensor_tensor(out=w, in0=w, scalar=0xF, in1=nib[:], op0=ALU.bitwise_and,
                                       op1=ALU.bitwise_or).then_inc(dq_bits, 1)
                dve.wait_ge(dq_bits, k5 + 2)
                V.tensor_scalar(nib[:], w, 9, 0x0E000E00, ALU.logical_shift_left,
                                ALU.bitwise_and).then_inc(dq_bits, 1)
                V.tensor_scalar(w, w, 12, -0x7FFF8000, ALU.logical_shift_left,
                                ALU.bitwise_and).then_inc(dq_bits, 1)
                dve.wait_ge(dq_bits, k5 + 4)
                V.tensor_tensor(nib[:], nib[:], w, ALU.bitwise_or).then_inc(dq_bits, 1)

            def unit_scale(k, u):
                dve.wait_ge(dq_bits, 5 * k + 5)
                dve.wait_ge(dq_lo, k)
                s = sc[:, bass.ds(u, 1), :].rearrange("p a w -> p w a")
                V.scalar_tensor_tensor(out=wf[:].rearrange("p a w -> p w a"),
                                       in0=nib[:].bitcast(F16).rearrange("p (w a) -> p w a", a=2),
                                       scalar=16384.0, in1=s.broadcast_to([P, 512, 2]),
                                       op0=ALU.mult, op1=ALU.mult).then_inc(dq_f, 1)

            def rope_of(b, c, t, ct):
                flat = "p a (h d) -> p (a h) d"
                dve.wait_ge(qk_silu, t + 1)
                dve.wait_ge(qkt_ps, t)
                if b is not None:
                    dve.wait_ge(kd_done, kvs(b, min(c + 1, CHUNKS - 1)))
                V.tensor_tensor(qr[:].rearrange(flat, d=HD), qa[:].rearrange(flat, d=HD),
                                rotT[:, 0, ct, :].unsqueeze(1).broadcast_to([P, 2 * HEADS, HD]),
                                ALU.mult).then_inc(rope_a, 1)

            stats(0)
            weight_lo(0, 0, 1)
            weight_lo(1, 1, 2)
            xt_lo_(0)
            dve.wait_ge(s_ghi, 5)
            V.tensor_tensor(g1l[:].rearrange("p k (r d) -> p k r d", r=4),
                            g1_in.unsqueeze(2).broadcast_to([P, KT, 4, HD]),
                            g1h[:].bitcast(F32).rearrange("p k (r d) -> p k r d", r=4),
                            ALU.subtract).then_inc(s_glo, 1)
            for r in (1, 3):
                V.tensor_tensor(g2s[32 * r:32 * r + 32, :], g2_in[32 * r:32 * r + 32, :],
                                g2s[32 * r:32 * r + 32, :].bitcast(F32),
                                ALU.subtract).then_inc(s_glo, 1)
            V.memset(st[:], 0.0).then_inc(s_st0, 1)
            silu_qk(0)
            gate_low(0)
            dve.wait_ge(s_tab, 16 * 5)
            rope_of(None, 0, 0, 0)
            xt_lo_(1)
            dve.wait_ge(s_w[3], 16)
            dve.wait_ge(s_nw, 16)
            for k in range(KT):
                ins = V.tensor_scalar(w_in[:, 0, 512 * k:512 * k + 512],
                                      w_in[:, 0, 512 * k:512 * k + 512], nw[:, k:k + 1], None,
                                      ALU.mult)
            ins.then_inc(s_wob, 1)

            def tile(b, c):
                t = CHUNKS * b + c
                if not at_start(b, c):
                    gated(t - 1)
                dve.wait_ge(qt_sb, t + 1)
                dve.wait_ge(o_ps, t)
                V.tensor_tensor(qdT[:], BS[0][:].rearrange("p (k t) -> p k t", k=KT), dqT[:],
                                ALU.mult).then_inc(qd_sb, 1)
                if not at_start(b, c):
                    normed(t - 1)
                if not near_end(b, c, 1):
                    silu_qk(t + 1)
                    gate_low(t + 1)
                if not at_start(b, c):
                    ot_lo_(t - 1)
                else:
                    weight_lo(3, 0, 4)
                if not near_end(b, c, 1):
                    rope_of(b, c, t + 1, (c + 1) % CHUNKS)
                for r in range(QB):
                    dve.wait_ge(score_ps, QB * t + r + 1)
                    V.tensor_tensor(pr[:, r, :], BS[r][:], maskT[:, r, :],
                                    ALU.mult).then_inc(prob_sb, 1)
                if not at_start(b, c):
                    add_x1(t - 1)
                if c < CHUNKS - 1:
                    dve.wait_ge(kv_ps, kvs(b, c) + 1)
                    if c:
                        dve.wait_ge(st_scaled, b * (CHUNKS - 2) + c)
                    else:
                        dve.wait_ge(inter_ps, b * (CHUNKS - 1))
                    for r in range(QB):
                        rows, cols = slice(32 * r, 32 * r + 32), slice(32 * r, 32 * r + 32)
                        kv = BK[rows, :].rearrange("p (g n) -> p g n", g=KT)[:, :, cols]
                        if c:
                            ins = V.tensor_tensor(st[rows, :, cols], st[rows, :, cols], kv, ALU.add)
                        else:
                            ins = V.tensor_copy(st[rows, :, cols], kv)
                    ins.then_inc(st_done, 1)
                if not near_end(b, c, 2):
                    xt_lo_(t + 2)
                if isinstance(b, int) and b == 0 and c in (0, 1, 3):
                    stats({0: 1, 1: 2, 3: 3}[c])
                if c == 2 and not near_end(b, c, 4):
                    unit_bits(b, b, [32] * UNITS)
                    unit_scale(b, b)

            batches(dve, tile)
            gated(TILES - 1)
            normed(TILES - 1)
            ot_lo_(TILES - 1)
            add_x1(TILES - 1)

            dve.wait_ge(bst_done, TILES)
            dve.wait_ge(x1_row, TILES)
            for t in range(TILES):
                V.bn_aggr(ln2[:, t, :], bst1[:, t, :]).then_inc(ln2_done, 1)
            dve.wait_ge(ln2_done, TILES)
            newton(s_ntl, ln2[:, :, 1], TILES, r2[:], NT * BATCH, 1.0, LN_EPS)

            def norm2(h, par):
                t = 2 * h + par
                src = acc[:, bass.ds(t, 1), :].rearrange("p a (j m n) -> p (a j) n m", j=2, n=2)
                if not (isinstance(t, int) and t < 2):
                    dve.wait_ge(x1t_ps, t - 1)
                V.tensor_scalar(wf[:, par, :].rearrange("p (j n m) -> p j n m", j=2, n=2), src,
                                ln2[:, bass.ds(t, 1), 0], r2[:, bass.ds(t, 1)],
                                ALU.subtract, ALU.mult).then_inc(n2_done, 1)

            def x1_lo(h, par):
                t = 2 * h + par
                dve.wait_ge(x1t_hi, t + 1)
                V.tensor_tensor(x1l[:, :, bass.ds(t * P, P)],
                                BX[par][:].rearrange("p (k t) -> p k t", k=KT),
                                x1h[:, :, bass.ds(t * P, P)].bitcast(F32),
                                ALU.subtract).then_inc(x1t_lo, 1)

            dve.wait_ge(dq_lo, UNITS)
            norm2(0, 0)
            norm2(0, 1)
            with dve.Fori(0, TILES // 2 - 1) as h:
                for par in range(2):
                    x1_lo(h, par)
                    norm2(h + 1, par)
            x1_lo(TILES // 2 - 1, 0)
            x1_lo(TILES // 2 - 1, 1)

            def add_y(s, tb):
                dve.wait_ge(y_ps[1], s + 1)
                for j in range(4):
                    row = acc[:, 4 * tb + j, :]
                    V.tensor_tensor(row, row, BY[j][:], ALU.add).then_inc(y_add, 1)

            def step(q, par_q, tb):
                s = TBS * q + tb
                dequant = tb >= 1 and not (isinstance(q, int) and q == BLOCKS - 1)
                k = UNITS * (q + 1) + tb - 1
                for par in range(2):
                    dve.wait_ge(h_sq[par], s + 1)
                    V.scalar_tensor_tensor(out=hx[par][:], in0=hx[par][:], scalar=1.0 / GELU_A,
                                           in1=BG[par][:], op0=ALU.add, op1=ALU.mult
                                           ).then_inc(h_arg[par], 1)
                    if par == 0 and dequant:
                        unit_bits(k, tb - 1, [32 * (q + 2) if n == tb - 1 else 0
                                              for n in range(UNITS)])
                    if par == 1 and dequant:
                        if tb == 1:
                            dve.wait_ge(y_ps[1], s - 1)
                        unit_scale(k, tb - 1)
                    dve.wait_ge(h_tanh[par], s + 1)
                    V.scalar_tensor_tensor(out=hx[par][:], in0=hx[par][:], scalar=1.0,
                                           in1=BG[par][:], op0=ALU.add, op1=ALU.mult
                                           ).then_inc(h_gelu[par], 1)
                    dve.wait_ge(h_gelu[par], s + 1)
                    dve.wait_ge(u_ps[par], s + 1)
                    V.scalar_tensor_tensor(out=hx[par][:], in0=hx[par][:], scalar=0.5,
                                           in1=BU[par][:], op0=ALU.mult, op1=ALU.mult
                                           ).then_inc(h_prod[par], 1)
                    if par == 0 and not (isinstance(s, int) and s == 0):
                        add_y(s - 1, (tb - 1) % TBS)
                    dve.wait_ge(h_hi[par], s + 1)
                    V.tensor_tensor(hl[par][:], hx[par][:], hh[par][:].bitcast(F32),
                                    ALU.subtract).then_inc(h_lo[par], 1)

            pairs(dve, step)
            add_y(TBS * BLOCKS - 1, TBS - 1)

        @block.gpsimd
        def _(pool):
            def rope_b_(t, c):
                pool.wait_ge(qk_silu, t + 1)
                pool.wait_ge(rope_c, t)
                half = "p a (h s d) -> p (a h) s d"
                for s in range(2):
                    ins = nc.gpsimd.tensor_tensor(
                        rb[:].rearrange(half, s=2, d=HD // 2)[:, :, s, :],
                        qa[:].rearrange(half, s=2, d=HD // 2)[:, :, 1 - s, :],
                        rotT[:, 1, c, 16 * s:16 * s + 16].unsqueeze(1)
                        .broadcast_to([P, 2 * HEADS, HD // 2]), ALU.mult)
                ins.then_inc(rope_b, 1)
                pool.wait_ge(rope_a, t + 1)
                pool.wait_ge(rope_b, t + 1)
                nc.gpsimd.tensor_tensor(qr[:], qr[:], rb[:], ALU.add).then_inc(rope_c, 1)

            def decay_k_(b, c, t):
                pool.wait_ge(rope_c, t + 1)
                pool.wait_ge(kv_ps, kvs(b, c))
                nc.gpsimd.tensor_tensor(kd[:].rearrange("p (h d) -> p h d", d=HD),
                                        qr[:, 1, :].rearrange("p (h d) -> p h d", d=HD),
                                        dkT[:].unsqueeze(2).broadcast_to([P, HEADS, HD]),
                                        ALU.mult).then_inc(kd_done, 1)

            def unit_lo(k, u, par):
                pool.wait_ge(dq_hi, k + 1)
                nc.gpsimd.tensor_tensor(
                    wl[par][:, bass.ds(u, 1), :].rearrange("p a w -> p (a w)"),
                    wf[:].rearrange("p a w -> p (a w)"),
                    wh[par][:, bass.ds(u, 1), :].rearrange("p a w -> p (a w)").bitcast(F32),
                    ALU.subtract).then_inc(dq_lo, 1)

            pool.wait_ge(s_whi, 3)
            nc.gpsimd.tensor_tensor(w_lo[2][:], w_in[:, 2, :].rearrange("p (k n) -> p k n", k=KT),
                                    w_hi[2][:].bitcast(F32), ALU.subtract).then_inc(s_vlo, 1)
            pool.wait_ge(s_tab, 16 * 5)
            pool.wait_ge(s_glo, 3)
            rope_b_(0, 0)
            decay_k_(0, 0, 0)

            def tile(b, c):
                t = CHUNKS * b + c
                if not near_end(b, c, 1):
                    rope_b_(t + 1, (c + 1) % CHUNKS)
                    if c == CHUNKS - 1:
                        decay_k_(b + 1, 0, t + 1)
                    elif c + 1 < CHUNKS - 1:
                        decay_k_(b, c + 1, t + 1)
                if 1 <= c < CHUNKS - 1:
                    pool.wait_ge(inter_ps, kvs(b, c))
                    pool.wait_ge(st_done, kvs(b, c))
                    nc.gpsimd.tensor_tensor(st[:], st[:], lamT[:].unsqueeze(2)
                                            .broadcast_to([P, KT, P]), ALU.mult
                                            ).then_inc(st_scaled, 1)
                if c == 2 and not near_end(b, c, 4):
                    unit_lo(b, b, 0)

            batches(pool, tile)

            def step(q, par_q, tb):
                if tb >= 1 and not (isinstance(q, int) and q == BLOCKS - 1):
                    unit_lo(UNITS * (q + 1) + tb - 1, tb - 1, 1 - par_q)

            pairs(pool, step)

        @block.tensor
        def _(pe):
            def split3(dst, ws, xs, start, stop):
                (w_h, w_l), (x_h, x_l) = ws, xs
                pe.matmul(dst, w_h, x_h, start=start, stop=False)
                pe.matmul(dst, w_h, x_l, start=False, stop=False)
                return pe.matmul(dst, w_l, x_h, start=False, stop=stop)

            def project(dst, n):
                for k in range(KT):
                    ins = split3(dst[:], (xth[:, k, :], xtl[:, k, :]),
                                 (w_hi[n][:, k, :], w_lo[n][:, k, :]), k == 0, k == KT - 1)
                return ins

            def transposes(dst, src):
                for k in range(KT):
                    ins = pe.transpose(dst[:, P * k:P * k + P], src[:, P * k:P * k + P], idt[:])
                return ins

            def x_transpose(t):
                pe.wait_ge(xn_done, t + 1)
                pe.wait_ge(v_sb, t)
                transposes(BV, xn).then_inc(xt_ps, 1)

            def qk_project(t):
                pe.wait_ge(xt_hi, t + 1)
                pe.wait_ge(xt_lo, t + 1)
                pe.wait_ge(qk_silu, t)
                if not (isinstance(t, int) and t < 3):
                    pe.wait_ge(x1_done, t - 2)
                project(BQ, 0)
                if isinstance(t, int) and t == 0:
                    pe.wait_ge(s_wlo, 2)
                project(BK, 1).then_inc(qk_ps, 1)

            def gate1(t):
                pe.wait_ge(gate_tanh, t)
                for k in range(KT):
                    ins = split3(BS[3][:, 0:P], (g1h[:, k, :], g1l[:, k, :]),
                                 (xth[:, k, :], xtl[:, k, :]), k == 0, k == KT - 1)
                ins.then_inc(g1_ps, 1)

            def v_project(t):
                project(BV, 2).then_inc(v_ps, 1)

            def gate2(t):
                pe.wait_ge(g_lo, t + 1)
                pe.wait_ge(prob_sb, QB * t)
                pe.matmul(BS[3][:], g4[:], g2s[:], start=True, stop=True).then_inc(gate_ps, 1)

            def o_transpose(t):
                pe.wait_ge(on_done, t + 1)
                transposes(BS[2], sq).then_inc(ot_ps, 1)

            def o_project(t):
                pe.wait_ge(ot_lo, t + 1)
                if not (isinstance(t, int) and t == 0):
                    pe.wait_ge(x1_done, t)
                for k in range(KT):
                    ins = split3(BQ[:], (oth[:, k, :], otl[:, k, :]),
                                 (w_hi[3][:, k, :], w_lo[3][:, k, :]), k == 0, k == KT - 1)
                ins.then_inc(wo_ps, 1)

            pe.wait_ge(s_id, 16)
            x_transpose(0)
            pe.wait_ge(s_wlo, 1)
            qk_project(0)
            pe.wait_ge(s_glo, 3)
            gate1(0)
            pe.wait_ge(s_vlo, 1)
            v_project(0)
            x_transpose(1)
            gate2(0)

            def tile(b, c):
                t = CHUNKS * b + c
                pe.wait_ge(rope_c, t + 1)
                transposes(BS[0], qr[:, 0, :])
                transposes(BS[1], qr[:, 1, :]).then_inc(qkt_ps, 1)
                if not at_start(b, c):
                    pe.wait_ge(st_done, kvs(b, c))
                if not near_end(b, c, 1):
                    qk_project(t + 1)
                    gate1(t + 1)
                if not at_start(b, c):
                    o_transpose(t - 1)
                if not near_end(b, c, 1):
                    v_project(t + 1)
                pe.wait_ge(qt_sb, t + 1)
                pe.wait_ge(kt_sb, t + 1)
                pe.wait_ge(qd_sb, t + 1)
                if not at_start(b, c):
                    pe.wait_ge(ot_lo, t)
                if not near_end(b, c, 1):
                    pe.wait_ge(g_lo, t + 2)
                else:
                    pe.wait_ge(gate_tanh, t + 1)
                for g in range(KT):
                    for r in range(QB):
                        ins = pe.matmul(BS[r][:, P * g:P * g + P], kT[32 * r:32 * r + 32, g, :],
                                        qT[32 * r:32 * r + 32, g, :], start=True, stop=True)
                        if g == KT - 1:
                            ins.then_inc(score_ps, 1)
                if not near_end(b, c, 1):
                    pe.wait_ge(qk_silu, t + 2)
                if not at_start(b, c):
                    if isinstance(b, int) and b == 0 and c == 1:
                        pe.wait_ge(s_wlo, 3)
                    o_project(t - 1)
                pe.wait_ge(v_sb, t + 1)
                if c < CHUNKS - 1:
                    pe.wait_ge(kd_done, kvs(b, c) + 1)
                    for g in range(KT):
                        ins = pe.matmul(BK[:, P * g:P * g + P], kd[:, P * g:P * g + P],
                                        vs[:, c % 2, P * g:P * g + P], start=True, stop=True)
                    ins.then_inc(kv_ps, 1)
                if not near_end(b, c, 2):
                    x_transpose(t + 2)
                if not at_start(b, c):
                    pe.wait_ge(xg_done, t)
                if c:
                    pe.wait_ge(st_done, kvs(b, c))
                    for g in range(KT):
                        ins = pe.matmul(BO[:, P * g:P * g + P], qdT[:, g, :], st[:, g, :],
                                        start=(g == 0), stop=False, skip_group_check=True)
                    ins.then_inc(inter_ps, 1)
                for r in range(QB):
                    pe.wait_ge(prob_sb, QB * t + r + 1)
                    for g in range(KT):
                        h = QB * g + r
                        ins = pe.matmul(BO[:, HD * h:HD * h + HD], pr[:, r, P * g:P * g + P],
                                        vs[:, c % 2, HD * h:HD * h + HD],
                                        start=(c == 0 and r == 0 and g == 0),
                                        stop=(r == QB - 1 and g == KT - 1), skip_group_check=True)
                ins.then_inc(o_ps, 1)
                if not near_end(b, c, 1):
                    gate2(t + 1)

            batches(pe, tile)
            o_transpose(TILES - 1)
            o_project(TILES - 1)

            def x1_transpose(t, par):
                pe.wait_ge(n2_done, t + 1)
                if not (isinstance(t, int) and t < 2):
                    pe.wait_ge(x1t_lo, t - 1)
                transposes(BX[par], wf[:, par, :]).then_inc(x1t_ps, 1)

            x1_transpose(0, 0)
            x1_transpose(1, 1)
            with pe.Fori(1, TILES // 2) as h:
                for par in range(2):
                    x1_transpose(2 * h + par, par)

            def gate_up(q, par_q, tb, par):
                s = TBS * q + tb
                pe.wait_ge(h_prod[par], s)
                for u, dst, done in ((GATE, BG[par], g_ps[par]), (UP, BU[par], u_ps[par])):
                    for k in range(KT):
                        cols = slice(512 * (k % 2) + 256 * (k // 2) + P * par,
                                     512 * (k % 2) + 256 * (k // 2) + P * par + P)
                        rows = slice(TB * tb, TB * tb + TB)
                        ins = split3(dst[:], (wh[par_q][:, u, cols], wl[par_q][:, u, cols]),
                                     (x1h[:, k, rows], x1l[:, k, rows]), k == 0, k == KT - 1)
                    ins.then_inc(done, 1)

            def down(s, par_q, par):
                pe.wait_ge(h_hi[par], s + 1)
                pe.wait_ge(h_lo[par], s + 1)
                if par == 0:
                    pe.wait_ge(y_add, 4 * s)
                for j in range(4):
                    if isinstance(s, int) and s == 0 and par == 0 and j == 2:
                        pe.wait_ge(x1t_lo, TILES)
                    ins = split3(BY[j][:], (hh[par][:, P * j:P * j + P], hl[par][:, P * j:P * j + P]),
                                 (wh[par_q][:, DOWN, 512 * par:512 * par + 512],
                                  wl[par_q][:, DOWN, 512 * par:512 * par + 512]),
                                 par == 0, par == 1)
                ins.then_inc(y_ps[par], 1)

            def step(q, par_q, tb):
                s = TBS * q + tb
                if isinstance(q, int) and q == 0:
                    pe.wait_ge(x1t_lo, 4 * (tb + 1))
                if tb == 0:
                    pe.wait_ge(dq_lo, UNITS * (q + 1))
                gate_up(q, par_q, tb, 0)
                if not (isinstance(s, int) and s == 0):
                    down(s - 1, par_q if tb else 1 - par_q, 1)
                gate_up(q, par_q, tb, 1)
                down(s, par_q, 0)

            pairs(pe, step)
            down(TBS * BLOCKS - 1, 1, 1)


def pairs(eng, step):
    def pair(n):
        for par_q in range(2):
            for tb in range(TBS):
                step(2 * n + par_q, par_q, tb)

    pair(0)
    with eng.Fori(1, BLOCKS // 2 - 1) as n:
        pair(n)
    pair(BLOCKS // 2 - 1)


def lay_out(inputs):
    def wide(w, last):
        return w.reshape(BLOCKS, P, 2, 2, last).transpose(0, 4, 3, 2, 1).reshape(BLOCKS, last, 512)

    packed = np.stack([wide(inputs["L0_ffn_gate_W_packed"], P), wide(inputs["L0_ffn_up_W_packed"], P),
                       inputs["L0_ffn_down_W_packed"].T.reshape(BLOCKS, P, 512)], axis=1)
    scales = np.stack([wide(inputs["L0_ffn_gate_scales"], 8), wide(inputs["L0_ffn_up_scales"], 8),
                       inputs["L0_ffn_down_scales"].T.reshape(BLOCKS, 8, 512)], axis=1)
    return {
        "x": inputs["L0_attn_x"], "wq": inputs["L0_attn_Wq"], "wk": inputs["L0_attn_Wk"],
        "wv": inputs["L0_attn_Wv"], "wo": inputs["L0_attn_Wo"], "wg1": inputs["L0_attn_Wg1"],
        "wg2": inputs["L0_attn_Wg2"], "norm_w": inputs["L0_attn_norm_weight"].reshape(KT, P).T,
        "packed": packed.reshape(BLOCKS * UNITS, P, 512),
        "scales": scales.reshape(BLOCKS * UNITS, 8, 512),
    } | shape_constants()


def kernel(**inputs):
    import concourse.bacc as bacc
    from concourse.bass_utils import run_bass_kernel_spmd

    arrays = {n: np.ascontiguousarray(a)
              for n, a in lay_out({n: np.asarray(a) for n, a in inputs.items()}).items()}
    nc = bacc.Bacc("TRN2", target_bir_lowering=False, num_devices=1)
    args = {n: nc.dram_tensor(n + "_dram", a.shape, mybir.dt.from_np(a.dtype),
                              kind="ExternalInput").ap() for n, a in arrays.items()}
    out = nc.dram_tensor("out_dram", (BATCH, SEQ, EMBED), F32, kind="ExternalOutput").ap()
    build(nc, out=out, **args)
    r = run_bass_kernel_spmd(nc, [{n + "_dram": a for n, a in arrays.items()}], core_ids=[0])
    return r.results[0]["out_dram"]
```

```python
from contextlib import ExitStack

import numpy as np

import concourse.bass as bass
from concourse import mybir
from concourse.alu_op_type import AluOpType as ALU

ACT = mybir.ActivationFunctionType
F32 = mybir.dt.float32
F32R = mybir.dt.float32r
F16 = mybir.dt.float16
I32 = mybir.dt.int32

P = 128
BATCH, SEQ, EMBED = 4, 512, 512
HEADS, HD = 16, 32
MLP = 4096
KT = EMBED // P
CHUNKS = SEQ // P
TILES = BATCH * CHUNKS
QB = 4
BLK = 256
BLOCKS = MLP // BLK
UNITS = 3
TB = 512
TBS = TILES * P // TB
LN_EPS, RMS_EPS = 1e-5, 1e-6
GELU_C, GELU_A = 0.7978845608028654, 0.044715
RSQRT_SEED = 1597463007.0
GATE, UP, DOWN = range(UNITS)


def shape_constants():
    f = np.float32
    half = HD // 2
    theta = np.power(f(10000.0), f(-2.0) * np.arange(half, dtype=f) / f(HD)).astype(f)
    ang = np.arange(SEQ, dtype=f)[:, None] * theta[None, :]
    cos, sin = np.cos(ang.astype(np.float64)), np.sin(ang.astype(np.float64))
    rot = np.stack([np.concatenate([cos, cos], 1), np.concatenate([-sin, sin], 1)], 0) * 0.5
    rot = rot.reshape(2, CHUNKS, P, HD).transpose(2, 0, 1, 3).astype(f)
    lam = -(2.0 ** (-8.0 * (np.arange(HEADS) + 1.0) / HEADS)).astype(f).astype(np.float64)
    i = np.arange(P)
    diff = (i[None, :] - i[:, None]).astype(np.float64)
    mask = np.where(diff[None] >= 0, np.exp(lam[:, None, None] * np.maximum(diff[None], 0)), 0.0)
    mask = mask.reshape(KT, QB, P, P).transpose(2, 1, 0, 3).astype(f)
    decay_q = np.exp(lam[:, None] * (i[None, :] + 1.0)).reshape(KT, QB, P)
    decay_q = np.repeat(decay_q.transpose(1, 0, 2), HD, axis=0).astype(f)
    decay_k = np.exp(lam[None, :] * (P - 1.0 - i[:, None])).astype(f)
    lam_c = np.repeat(np.exp(lam * P).reshape(KT, QB).T, HD, axis=0).astype(f)
    c = np.ascontiguousarray
    return {"rot": c(rot), "mask": c(mask), "decay_q": c(decay_q), "decay_k": c(decay_k),
            "lam_c": c(lam_c), "ident": np.eye(P, dtype=f)}


def build(nc, x, wq, wk, wv, wo, wg1, wg2, norm_w, packed, scales,
          rot, mask, decay_q, decay_k, lam_c, ident, out):
    ctx = ExitStack()
    with ctx:
        def sb(name, shape, dt=F32, scope=ctx):
            return scope.enter_context(nc.sbuf_tensor(name, shape, dt))

        def sem(name):
            return ctx.enter_context(nc.semaphore(name))

        acc = sb("acc", [P, TILES, EMBED])
        idt = sb("idt", [P, P])
        pk = sb("pk", [P, UNITS, 512], I32)
        sc = sb("sc", [P, UNITS, 512])
        nib = sb("nib", [P, 512], I32)
        wf = sb("wf", [P, 2, 512])
        ln1 = sb("ln1", [P, TILES, 2])
        ln2 = sb("ln2", [P, TILES, 2])
        r1 = sb("r1", [P, TILES])
        nm1 = sb("nm1", [P, TILES])
        r2 = sb("r2", [P, TILES])
        nm2 = sb("nm2", [P, TILES])
        nt_v = sb("nt_v", [P, 16])
        nt_t = sb("nt_t", [P, 16])
        bst = sb("bst", [P, 6])
        bst1 = sb("bst1", [P, TILES, 6])
        with ExitStack() as early:
            w_in = sb("w_in", [P, 3, KT * 512], F32, early)
        wh0 = sb("wh0", [P, UNITS, 1024], F32R)
        wl0 = sb("wl0", [P, UNITS, 1024], F32R)
        with ExitStack() as att_w:
            w_hi = [sb(f"w_hi{n}", [P, KT, 512], F32R, att_w) for n in range(4)]
            w_lo = [sb(f"w_lo{n}", [P, KT, 512], F32R, att_w) for n in range(4)]
        x1h = sb("x1h", [P, TBS, KT, TB], F32R)
        x1l = sb("x1l", [P, TBS, KT, TB], F32R)
        with ExitStack() as att:
            g1h = sb("g1h", [P, KT, P], F32R, att)
            g1l = sb("g1l", [P, KT, P], F32R, att)
            g2s = sb("g2s", [P, 512], F32R, att)
            nw = sb("nw", [P, KT], F32, att)
            rotT = sb("rotT", [P, 2, CHUNKS, HD], F32, att)
            maskT = sb("maskT", [P, QB, 512], F32, att)
            dqT = sb("dqT", [P, KT, P], F32, att)
            dkT = sb("dkT", [P, HEADS], F32, att)
            lamT = sb("lamT", [P, KT], F32, att)
            xn = sb("xn", [P, 512], F32, att)
            xth = sb("xth", [P, KT, P], F32R, att)
            xtl = sb("xtl", [P, KT, P], F32R, att)
            qa = sb("qa", [P, 2, 512], F32, att)
            rb = sb("rb", [P, 2, 512], F32, att)
            qr = sb("qr", [P, 2, 512], F32, att)
            g1_in = rb[:, 1, 0:KT * HD].rearrange("p (k d) -> p k d", k=KT)
            g2_in = rb[:, 0, :]
            kd = sb("kd", [P, 512], F32, att)
            qT = sb("qT", [P, KT, P], F32, att)
            kT = sb("kT", [P, KT, P], F32, att)
            qdT = sb("qdT", [P, KT, P], F32, att)
            g4 = sb("g4", [P, P], F32R, att)
            g4h = sb("g4h", [P, P], F32R, att)
            vs = sb("vs", [P, 2, 512], F32, att)
            tg = sb("tg", [P, 512], F32, att)
            pr = sb("pr", [P, QB, 512], F32, att)
            st = sb("st", [P, KT, P], F32, att)
            xg = sb("xg", [P, 512], F32, att)
            sq = sb("sq", [P, 512], F32, att)
            oth = sb("oth", [P, KT, P], F32R, att)
            otl = sb("otl", [P, KT, P], F32R, att)
            ms = sb("ms", [P, HEADS], F32, att)
            rr = sb("rr", [P, HEADS], F32, att)
        wh1 = sb("wh1", [P, UNITS, 1024], F32R)
        wl1 = sb("wl1", [P, UNITS, 1024], F32R)
        hx = [sb(f"hx{n}", [P, 512]) for n in range(2)]
        hh = [sb(f"hh{n}", [P, 512], F32R) for n in range(2)]
        hl = [sb(f"hl{n}", [P, 512], F32R) for n in range(2)]
        wh, wl = [wh0, wh1], [wl0, wl1]

        bank = [ctx.enter_context(nc.psum_tensor(f"bank{n}", [P, 512], F32)) for n in range(8)]
        BQ, BK, BS, BV, BO = bank[0], bank[1], bank[2:6], bank[6], bank[7]
        BG, BU, BY = bank[0:4:2], bank[1:4:2], bank[4:8]
        BX = [bank[n] for n in (1, 6, 1, 6, 5, 6, 5, 6, 5, 6, 7, 6, 4, 5, 6, 7)]

        s_x = [sem(f"s_x{b}") for b in range(BATCH)]
        s_nw = sem("s_nw")
        s_id = sem("s_id")
        s_w = [sem(f"s_w{n}") for n in range(4)]
        s_small = sem("s_small")
        s_tab = sem("s_tab")
        s_unit = [sem(f"s_unit{u}") for u in range(UNITS)]
        s_out = sem("s_out")
        s_whi = sem("s_whi")
        s_wlo = sem("s_wlo")
        s_wob = sem("s_wob")
        s_ghi = sem("s_ghi")
        s_glo = sem("s_glo")
        s_bn1 = sem("s_bn1")
        s_ln1 = sem("s_ln1")
        s_nt = sem("s_nt")
        s_ntl = sem("s_ntl")
        s_r1 = sem("s_r1")
        s_r2 = sem("s_r2")
        s_vlo = sem("s_vlo")
        s_st0 = sem("s_st0")
        xn_done = sem("xn_done")
        xt_ps, xt_hi, xt_lo = sem("xt_ps"), sem("xt_hi"), sem("xt_lo")
        qk_ps, g1_ps, v_ps, gate_ps = sem("qk_ps"), sem("g1_ps"), sem("v_ps"), sem("gate_ps")
        g_hi, g_lo = sem("g_hi"), sem("g_lo")
        qk_tanh, qk_silu = sem("qk_tanh"), sem("qk_silu")
        v_sb, gate_tanh = sem("v_sb"), sem("gate_tanh")
        rope_a, rope_b, rope_c = sem("rope_a"), sem("rope_b"), sem("rope_c")
        kd_done = sem("kd_done")
        qkt_ps, qt_sb, kt_sb, qd_sb = sem("qkt_ps"), sem("qt_sb"), sem("kt_sb"), sem("qd_sb")
        score_ps, prob_sb = sem("score_ps"), sem("prob_sb")
        inter_ps, o_ps, kv_ps = sem("inter_ps"), sem("o_ps"), sem("kv_ps")
        st_scaled, st_done = sem("st_scaled"), sem("st_done")
        xg_done, sq_done, ms_done, on_done = (sem("xg_done"), sem("sq_done"), sem("ms_done"),
                                              sem("on_done"))
        ot_ps, ot_hi, ot_lo, wo_ps = sem("ot_ps"), sem("ot_hi"), sem("ot_lo"), sem("wo_ps")
        x1_done, x1_row, bn_done = sem("x1_done"), sem("x1_row"), sem("bn_done")
        bst_done, ln2_done = sem("bst_done"), sem("ln2_done")
        dq_bits, dq_f, dq_hi, dq_lo = sem("dq_bits"), sem("dq_f"), sem("dq_hi"), sem("dq_lo")
        n2_done = sem("n2_done")
        x1t_ps, x1t_hi, x1t_lo = sem("x1t_ps"), sem("x1t_hi"), sem("x1t_lo")
        g_ps = [sem(f"g_ps{n}") for n in range(2)]
        u_ps = [sem(f"u_ps{n}") for n in range(2)]
        h_sq = [sem(f"h_sq{n}") for n in range(2)]
        h_arg = [sem(f"h_arg{n}") for n in range(2)]
        h_tanh = [sem(f"h_tanh{n}") for n in range(2)]
        h_gelu = [sem(f"h_gelu{n}") for n in range(2)]
        h_prod = [sem(f"h_prod{n}") for n in range(2)]
        h_hi = [sem(f"h_hi{n}") for n in range(2)]
        h_lo = [sem(f"h_lo{n}") for n in range(2)]
        y_ps = [sem(f"y_ps{n}") for n in range(2)]
        y_add = sem("y_add")

        NT = 11

        def batches(eng, body, last_tile):
            for c in range(CHUNKS):
                body(0, c)
            with eng.Fori(1, BATCH - 1) as b:
                for c in range(CHUNKS):
                    body(b, c)
            for c in range(CHUNKS - 1):
                body(BATCH - 1, c)
            last_tile()

        def near_end(b, c, ahead):
            return isinstance(b, int) and b * CHUNKS + c + ahead >= TILES

        def at_start(b, c):
            return isinstance(b, int) and b == 0 and c == 0

        def kvs(b, c):
            return b * (CHUNKS - 1) + c

        block = ctx.enter_context(nc.Block())

        @block.sync
        def _(sp):
            xv = x.rearrange("b (c p) d -> p (b c) d", p=P)
            w_view = [w.rearrange("(k p) n -> p k n", p=P) for w in (wq, wk, wv, wo)]

            def load_x(b):
                sp.dma_start(acc[:, 4 * b:4 * b + 4, :], xv[:, 4 * b:4 * b + 4, :]
                             ).then_inc(s_x[b], 16)

            def load_w(n, slot):
                sp.dma_start(w_in[:, slot, :].rearrange("p (k n) -> p k n", k=KT),
                             w_view[n]).then_inc(s_w[n], 16)

            load_x(0)
            sp.dma_start(idt[:], ident).then_inc(s_id, 16)
            load_w(0, 0)
            load_w(1, 1)
            sp.dma_start(g1_in, wg1.rearrange("(k p) n -> p k n", p=P)).then_inc(s_small, 16)
            for r in range(4):
                sp.dma_start(g2_in[32 * r:32 * r + 32, :], wg2).then_inc(s_small, 16)
            load_w(2, 2)
            sp.dma_start(rotT[:], rot).then_inc(s_tab, 16)
            sp.dma_start(maskT[:], mask.rearrange("p r g t -> p r (g t)")).then_inc(s_tab, 16)
            sp.dma_start(dqT[:], decay_q).then_inc(s_tab, 16)
            sp.dma_start(dkT[:], decay_k).then_inc(s_tab, 16)
            sp.dma_start(lamT[:], lam_c).then_inc(s_tab, 16)
            for b in range(1, BATCH):
                load_x(b)
            sp.dma_start(nw[:], norm_w).then_inc(s_nw, 16)
            sp.wait_ge(s_whi, 1)
            sp.wait_ge(s_wlo, 1)
            load_w(3, 0)

            def load_unit(q, u):
                sp.dma_start(pk[:, u, :], packed[bass.ds(q * UNITS + u, 1), :, :]
                             .rearrange("a p w -> p (a w)")).then_inc(s_unit[u], 16)
                src = scales[bass.ds(q * UNITS + u, 1), :, :].rearrange("a r w -> (a r) w")
                sp.dma_start(sc[:, u, :], src.unsqueeze(1).broadcast_to([8, 16, 512])
                             ).then_inc(s_unit[u], 16)

            for u in range(UNITS):
                load_unit(0, u)
            with sp.Fori(1, BLOCKS) as q:
                for u in range(UNITS):
                    sp.wait_ge(dq_f, q * UNITS - UNITS + u + 1)
                    load_unit(q, u)
            ov = out.rearrange("b (c p) d -> p (b c) d", p=P)
            for tb in range(TBS):
                for j in range(4):
                    sp.wait_ge(y_add, 4 * (TBS * (BLOCKS - 1) + tb) + j + 1)
                    sp.dma_start(ov[:, 4 * tb + j, :], acc[:, 4 * tb + j, :]
                                 ).then_inc(s_out, 16)
            sp.wait_ge(s_out, 16 * TILES)

        @block.scalar
        def _(act):
            A = nc.scalar.activation

            def weight_hi(n, slot):
                act.wait_ge(s_w[n], 16)
                A(w_hi[n][:], w_in[:, slot, :].rearrange("p (k n) -> p k n", k=KT),
                  ACT.Copy).then_inc(s_whi, 1)

            def norm1(t, ln):
                act.wait_ge(s_r1, ln)
                act.wait_ge(xt_ps, t)
                A(xn[:], acc[:, bass.ds(t, 1), :].rearrange("p a d -> p (a d)"), ACT.Identity,
                  bias=nm1[:, bass.ds(t, 1)], scale=r1[:, bass.ds(t, 1)]).then_inc(xn_done, 1)

            def xt_hi_(t):
                act.wait_ge(xt_ps, t + 1)
                act.wait_ge(v_ps, t)
                A(xth[:], BV[:].rearrange("p (k t) -> p k t", k=KT), ACT.Copy).then_inc(xt_hi, 1)

            def gate_low(t):
                act.wait_ge(g1_ps, t + 1)
                act.wait_ge(gate_ps, t)
                A(g4h[64:128, :], BS[3][64:128, 0:P], ACT.Copy)
                A(g4[0:64, :], BS[3][0:64, 0:P], ACT.Copy).then_inc(g_hi, 1)

            def tanh_qk(t):
                act.wait_ge(qk_ps, t + 1)
                act.wait_ge(qk_silu, t)
                if not (isinstance(t, int) and t == 0):
                    act.wait_ge(rope_c, t)
                A(qa[:, 0, :], BQ[:], ACT.Tanh, scale=0.5)
                A(qa[:, 1, :], BK[:], ACT.Tanh, scale=0.5).then_inc(qk_tanh, 1)

            def v_copy(t, par):
                act.wait_ge(v_ps, t + 1)
                if not (isinstance(t, int) and t < 2):
                    act.wait_ge(o_ps, t - 1)
                A(vs[:, par, :], BV[:], ACT.Copy).then_inc(v_sb, 1)

            def tanh_gate(t):
                act.wait_ge(gate_ps, t + 1)
                act.wait_ge(xg_done, t)
                A(tg[:], BS[3][:], ACT.Tanh, scale=0.5).then_inc(gate_tanh, 1)

            def square(t):
                act.wait_ge(xg_done, t + 1)
                act.wait_ge(ot_ps, t)
                A(sq[:], xg[:], ACT.Square).then_inc(sq_done, 1)

            def ot_hi_(t):
                act.wait_ge(ot_ps, t + 1)
                act.wait_ge(wo_ps, t)
                A(oth[:], BO[:].rearrange("p (k t) -> p k t", k=KT), ACT.Copy).then_inc(ot_hi, 1)

            def unit_hi(k, u, par):
                act.wait_ge(dq_f, k + 1)
                A(wh[par][:, bass.ds(u, 1), :].rearrange("p a w -> p (a w)"),
                  wf[:].rearrange("p a w -> p (a w)"), ACT.Copy).then_inc(dq_hi, 1)

            weight_hi(0, 0)
            norm1(0, 1)
            weight_hi(1, 1)
            xt_hi_(0)
            weight_hi(2, 2)
            norm1(1, 1)
            act.wait_ge(s_small, 16 * 5)
            A(g1h[:].rearrange("p k (r d) -> p k r d", r=4),
              g1_in.unsqueeze(2).broadcast_to([P, KT, 4, HD]), ACT.Copy).then_inc(s_ghi, 1)
            for r in range(4):
                A(g2s[32 * r:32 * r + 32, :], g2_in[32 * r:32 * r + 32, :],
                  ACT.Copy).then_inc(s_ghi, 1)
            tanh_qk(0)
            gate_low(0)
            v_copy(0, 0)
            xt_hi_(1)
            norm1(2, 1)
            tanh_gate(0)
            act.wait_ge(s_wob, 1)
            A(w_hi[3][:], w_in[:, 0, :].rearrange("p (k n) -> p k n", k=KT),
              ACT.Copy).then_inc(s_whi, 1)

            def tile(b, c):
                t = CHUNKS * b + c
                act.wait_ge(qkt_ps, t + 1)
                act.wait_ge(score_ps, QB * t)
                A(qT[:], BS[0][:].rearrange("p (k t) -> p k t", k=KT), ACT.Copy).then_inc(qt_sb, 1)
                A(kT[:], BS[1][:].rearrange("p (k t) -> p k t", k=KT), ACT.Copy).then_inc(kt_sb, 1)
                if not at_start(b, c):
                    square(t - 1)
                if c == 3 and not near_end(b, c, 1):
                    unit_hi(b, b, 0)
                if not near_end(b, c, 1):
                    tanh_qk(t + 1)
                    gate_low(t + 1)
                if not at_start(b, c):
                    ot_hi_(t - 1)
                if not near_end(b, c, 1):
                    v_copy(t + 1, (c + 1) % 2)
                if not near_end(b, c, 2):
                    xt_hi_(t + 2)
                if not near_end(b, c, 3):
                    ahead = (c + 3) // CHUNKS + 1
                    norm1(t + 3, b + ahead)
                if not near_end(b, c, 1):
                    tanh_gate(t + 1)
            def x1t_hi_(t):
                act.wait_ge(x1t_ps, t + 1)
                A(x1h[:, t // 4, :, P * (t % 4):P * (t % 4) + P],
                  BX[t][:].rearrange("p (k t) -> p k t", k=KT), ACT.Copy).then_inc(x1t_hi, 1)

            def last_tile():
                t = TILES - 1
                act.wait_ge(qkt_ps, t + 1)
                act.wait_ge(score_ps, QB * t)
                A(qT[:], BS[0][:].rearrange("p (k t) -> p k t", k=KT), ACT.Copy).then_inc(qt_sb, 1)
                A(kT[:], BS[1][:].rearrange("p (k t) -> p k t", k=KT), ACT.Copy).then_inc(kt_sb, 1)
                square(t - 1)
                x1t_hi_(0)
                x1t_hi_(1)
                ot_hi_(t - 1)
                x1t_hi_(2)
                x1t_hi_(3)
                square(t)
                x1t_hi_(4)
                x1t_hi_(5)

            batches(act, tile, last_tile)

            def step(q, par_q, tb):
                s = TBS * q + tb
                at = s if isinstance(s, int) else None
                for par in range(2):
                    act.wait_ge(g_ps[par], s + 1)
                    act.wait_ge(h_lo[par], s)
                    A(hx[par][:], BG[par][:], ACT.Square).then_inc(h_sq[par], 1)
                    act.wait_ge(h_arg[par], s + 1)
                    A(hx[par][:], hx[par][:], ACT.Tanh, scale=GELU_C * GELU_A
                      ).then_inc(h_tanh[par], 1)
                    if at == 0 and par == 0:
                        ot_hi_(TILES - 1)
                    if par == 1 and tb >= 1 and not (isinstance(q, int) and q == BLOCKS - 1) and at != 1:
                        unit_hi(UNITS * (q + 1) + tb - 1, tb - 1, 1 - par_q)
                    act.wait_ge(h_prod[par], s + 1)
                    act.wait_ge(y_ps[par], s)
                    A(hh[par][:], hx[par][:], ACT.Copy).then_inc(h_hi[par], 1)
                    if at == 0 and par == 0:
                        x1t_hi_(6)
                        x1t_hi_(7)
                if at == 0:
                    for t in range(8, 12):
                        x1t_hi_(t)
                if at == 1:
                    for t in range(12, TILES):
                        x1t_hi_(t)
                    unit_hi(UNITS, 0, 1)

            pairs(act, step)

        @block.vector
        def _(dve):
            V = nc.vector

            def newton(steps, v, n, r, base, scale, eps):
                vv, tt = nt_v[:, 0:n], nt_t[:, 0:n]
                k = [0]

                def done(ins):
                    k[0] += 1
                    ins.then_inc(steps, 1)
                    dve.wait_ge(steps, base + k[0])

                done(V.tensor_scalar(vv, v, scale, eps, ALU.mult, ALU.add))
                done(V.tensor_scalar(r.bitcast(I32), vv.bitcast(I32), -0.5, RSQRT_SEED,
                                     ALU.mult, ALU.add))
                for _ in range(3):
                    done(V.scalar_tensor_tensor(out=tt, in0=r, scalar=-0.5, in1=r,
                                                op0=ALU.mult, op1=ALU.mult))
                    done(V.tensor_tensor(tt, tt, vv, ALU.mult))
                    done(V.scalar_tensor_tensor(out=r, in0=tt, scalar=1.5, in1=r,
                                                op0=ALU.add, op1=ALU.mult))
                assert k[0] == NT

            def stats(b):
                dve.wait_ge(s_x[b], 16)
                for t in range(CHUNKS * b, CHUNKS * b + CHUNKS):
                    V.bn_stats(bst1[:, t, :], acc[:, t, :]).then_inc(s_bn1, 1)

            def stats_r(b):
                rows = slice(CHUNKS * b, CHUNKS * b + CHUNKS)
                for t in range(CHUNKS * b, CHUNKS * b + CHUNKS):
                    dve.wait_ge(s_bn1, t + 1)
                    V.bn_aggr(ln1[:, t, :], bst1[:, t, :]).then_inc(s_ln1, 1)
                dve.wait_ge(s_ln1, CHUNKS * b + CHUNKS)
                newton(s_ntl, ln1[:, rows, 1], CHUNKS, r1[:, rows], NT * b, 1.0, LN_EPS)
                V.scalar_tensor_tensor(out=nm1[:, rows], in0=ln1[:, rows, 0], scalar=-1.0,
                                       in1=r1[:, rows], op0=ALU.mult, op1=ALU.mult
                                       ).then_inc(s_r1, 1)

            def weight_lo(n, slot, his):
                dve.wait_ge(s_whi, his)
                V.tensor_tensor(w_lo[n][:], w_in[:, slot, :].rearrange("p (k n) -> p k n", k=KT),
                                w_hi[n][:].bitcast(F32), ALU.subtract).then_inc(s_wlo, 1)

            def xt_lo_(t):
                dve.wait_ge(xt_hi, t + 1)
                V.tensor_tensor(xtl[:], BV[:].rearrange("p (k t) -> p k t", k=KT),
                                xth[:].bitcast(F32), ALU.subtract).then_inc(xt_lo, 1)

            def gate_low(t):
                dve.wait_ge(g_hi, t + 1)
                V.tensor_tensor(g4[64:128, :], BS[3][64:128, 0:P], g4h[64:128, :].bitcast(F32),
                                ALU.subtract).then_inc(g_lo, 1)

            def silu_qk(t):
                dve.wait_ge(qk_tanh, t + 1)
                V.scalar_tensor_tensor(out=qa[:, 0, :], in0=qa[:, 0, :], scalar=1.0, in1=BQ[:],
                                       op0=ALU.add, op1=ALU.mult)
                V.scalar_tensor_tensor(out=qa[:, 1, :], in0=qa[:, 1, :], scalar=1.0, in1=BK[:],
                                       op0=ALU.add, op1=ALU.mult).then_inc(qk_silu, 1)

            def gated(t):
                dve.wait_ge(o_ps, t + 1)
                dve.wait_ge(gate_tanh, t + 1)
                dve.wait_ge(on_done, t)
                V.scalar_tensor_tensor(out=xg[:], in0=tg[:], scalar=1.0, in1=BO[:],
                                       op0=ALU.add, op1=ALU.mult).then_inc(xg_done, 1)

            def normed(t):
                dve.wait_ge(sq_done, t + 1)
                V.tensor_reduce(ms[:], sq[:].rearrange("p (h d) -> p h d", d=HD),
                                mybir.AxisListType.X, ALU.add).then_inc(ms_done, 1)
                dve.wait_ge(ms_done, t + 1)
                newton(s_nt, ms[:], HEADS, rr[:], NT * t, 1.0 / HD, 4 * RMS_EPS)
                V.tensor_tensor(sq[:].rearrange("p (h d) -> p h d", d=HD),
                                xg[:].rearrange("p (h d) -> p h d", d=HD),
                                rr[:].unsqueeze(2).broadcast_to([P, HEADS, HD]),
                                ALU.mult).then_inc(on_done, 1)

            def ot_lo_(t):
                dve.wait_ge(ot_hi, t + 1)
                V.tensor_tensor(otl[:], BO[:].rearrange("p (k t) -> p k t", k=KT),
                                oth[:].bitcast(F32), ALU.subtract).then_inc(ot_lo, 1)

            def add_x1(t):
                dve.wait_ge(wo_ps, t + 1)
                row = acc[:, bass.ds(t, 1), :].rearrange("p a d -> p (a d)")
                wo = BS[2] if isinstance(t, int) and t == TILES - 1 else BQ
                V.tensor_tensor(sq[:], row, wo[:], ALU.add).then_inc(x1_done, 1)
                dve.wait_ge(x1_done, t + 1)
                V.bn_stats(bst[:], sq[:]).then_inc(bn_done, 1)
                V.tensor_scalar(row, sq[:], 1.0, None, ALU.mult).then_inc(x1_row, 1)
                dve.wait_ge(bn_done, t + 1)
                V.tensor_scalar(bst1[:, bass.ds(t, 1), :].rearrange("p a d -> p (a d)"), bst[:],
                                1.0, None, ALU.mult).then_inc(bst_done, 1)

            def unit_bits(k, u, loads):
                w = pk[:, bass.ds(u, 1), :].rearrange("p a w -> p (a w)")
                for n, wait in enumerate(loads):
                    dve.wait_ge(s_unit[n], wait)
                k5 = 5 * k
                V.tensor_scalar(nib[:], w, 12, 0x000F0000, ALU.logical_shift_left,
                                ALU.bitwise_and).then_inc(dq_bits, 1)
                dve.wait_ge(dq_bits, k5 + 1)
                V.scalar_tensor_tensor(out=w, in0=w, scalar=0xF, in1=nib[:], op0=ALU.bitwise_and,
                                       op1=ALU.bitwise_or).then_inc(dq_bits, 1)
                dve.wait_ge(dq_bits, k5 + 2)
                V.tensor_scalar(nib[:], w, 9, 0x0E000E00, ALU.logical_shift_left,
                                ALU.bitwise_and).then_inc(dq_bits, 1)
                V.tensor_scalar(w, w, 12, -0x7FFF8000, ALU.logical_shift_left,
                                ALU.bitwise_and).then_inc(dq_bits, 1)
                dve.wait_ge(dq_bits, k5 + 4)
                V.tensor_tensor(nib[:], nib[:], w, ALU.bitwise_or).then_inc(dq_bits, 1)

            def unit_scale(k, u):
                dve.wait_ge(dq_bits, 5 * k + 5)
                dve.wait_ge(dq_lo, k)
                s = sc[:, bass.ds(u, 1), :].rearrange("p a w -> p w a")
                V.scalar_tensor_tensor(out=wf[:].rearrange("p a w -> p w a"),
                                       in0=nib[:].bitcast(F16).rearrange("p (w a) -> p w a", a=2),
                                       scalar=16384.0, in1=s.broadcast_to([P, 512, 2]),
                                       op0=ALU.mult, op1=ALU.mult).then_inc(dq_f, 1)

            def stats2(n):
                first, last = (0, TILES - CHUNKS) if n == 0 else (TILES - CHUNKS, TILES)
                rows = slice(first, last)
                dve.wait_ge(bst_done, last)
                dve.wait_ge(x1_row, last)
                for t in range(first, last):
                    V.bn_aggr(ln2[:, t, :], bst1[:, t, :]).then_inc(ln2_done, 1)
                dve.wait_ge(ln2_done, last)
                newton(s_ntl, ln2[:, rows, 1], last - first, r2[:, rows], NT * (BATCH + n), 1.0,
                       LN_EPS)
                V.scalar_tensor_tensor(out=nm2[:, rows], in0=ln2[:, rows, 0], scalar=-1.0,
                                       in1=r2[:, rows], op0=ALU.mult, op1=ALU.mult
                                       ).then_inc(s_r2, 1)

            def rope_of(b, c, t, ct):
                flat = "p a (h d) -> p (a h) d"
                dve.wait_ge(qk_silu, t + 1)
                dve.wait_ge(qkt_ps, t)
                if b is not None:
                    dve.wait_ge(kd_done, kvs(b, min(c + 1, CHUNKS - 1)))
                V.tensor_tensor(qr[:].rearrange(flat, d=HD), qa[:].rearrange(flat, d=HD),
                                rotT[:, 0, ct, :].unsqueeze(1).broadcast_to([P, 2 * HEADS, HD]),
                                ALU.mult).then_inc(rope_a, 1)

            stats(0)
            stats_r(0)
            weight_lo(0, 0, 1)
            xt_lo_(0)
            weight_lo(1, 1, 2)
            dve.wait_ge(s_ghi, 5)
            V.tensor_tensor(g1l[:].rearrange("p k (r d) -> p k r d", r=4),
                            g1_in.unsqueeze(2).broadcast_to([P, KT, 4, HD]),
                            g1h[:].bitcast(F32).rearrange("p k (r d) -> p k r d", r=4),
                            ALU.subtract).then_inc(s_glo, 1)
            for r in (1, 3):
                V.tensor_tensor(g2s[32 * r:32 * r + 32, :], g2_in[32 * r:32 * r + 32, :],
                                g2s[32 * r:32 * r + 32, :].bitcast(F32),
                                ALU.subtract).then_inc(s_glo, 1)
            V.memset(st[:], 0.0).then_inc(s_st0, 1)
            silu_qk(0)
            gate_low(0)
            dve.wait_ge(s_tab, 16 * 5)
            rope_of(None, 0, 0, 0)
            xt_lo_(1)
            dve.wait_ge(s_w[3], 16)
            dve.wait_ge(s_nw, 16)
            for k in range(KT):
                ins = V.tensor_scalar(w_in[:, 0, 512 * k:512 * k + 512],
                                      w_in[:, 0, 512 * k:512 * k + 512], nw[:, k:k + 1], None,
                                      ALU.mult)
            ins.then_inc(s_wob, 1)
            stats(1)
            stats_r(1)

            def tile(b, c):
                t = CHUNKS * b + c
                if not at_start(b, c):
                    gated(t - 1)
                dve.wait_ge(qt_sb, t + 1)
                dve.wait_ge(o_ps, t)
                V.tensor_tensor(qdT[:], BS[0][:].rearrange("p (k t) -> p k t", k=KT), dqT[:],
                                ALU.mult).then_inc(qd_sb, 1)
                if not at_start(b, c):
                    normed(t - 1)
                if not near_end(b, c, 1):
                    gate_low(t + 1)
                    silu_qk(t + 1)
                if not at_start(b, c):
                    ot_lo_(t - 1)
                else:
                    weight_lo(3, 0, 4)
                if not near_end(b, c, 1):
                    rope_of(b, c, t + 1, (c + 1) % CHUNKS)
                for r in range(QB):
                    dve.wait_ge(score_ps, QB * t + r + 1)
                    V.tensor_tensor(pr[:, r, :], BS[r][:], maskT[:, r, :],
                                    ALU.mult).then_inc(prob_sb, 1)
                if not near_end(b, c, 2):
                    xt_lo_(t + 2)
                if not at_start(b, c):
                    add_x1(t - 1)
                if c < CHUNKS - 1:
                    dve.wait_ge(kv_ps, kvs(b, c) + 1)
                    if c:
                        dve.wait_ge(st_scaled, b * (CHUNKS - 2) + c)
                    else:
                        dve.wait_ge(inter_ps, b * (CHUNKS - 1))
                    for r in range(QB):
                        rows, cols = slice(32 * r, 32 * r + 32), slice(32 * r, 32 * r + 32)
                        kv = BK[rows, :].rearrange("p (g n) -> p g n", g=KT)[:, :, cols]
                        if c:
                            ins = V.tensor_tensor(st[rows, :, cols], st[rows, :, cols], kv, ALU.add)
                        else:
                            ins = V.tensor_copy(st[rows, :, cols], kv)
                    ins.then_inc(st_done, 1)
                if isinstance(b, int) and b == 0:
                    if c in (0, 3):
                        stats({0: 2, 3: 3}[c])
                    if c in (1, 3):
                        stats_r({1: 2, 3: 3}[c])
                if c == 2 and not near_end(b, c, 4):
                    unit_bits(b, b, [32] * UNITS)
                    unit_scale(b, b)
                if isinstance(b, int) and b == BATCH - 1 and c == 1:
                    stats2(0)

            def x1t_lo_(t):
                dve.wait_ge(x1t_hi, t + 1)
                cols = slice(P * (t % 4), P * (t % 4) + P)
                V.tensor_tensor(x1l[:, t // 4, :, cols],
                                BX[t][:].rearrange("p (k t) -> p k t", k=KT),
                                x1h[:, t // 4, :, cols].bitcast(F32), ALU.subtract
                                ).then_inc(x1t_lo, 1)

            def last_tile():
                t = TILES - 1
                gated(t - 1)
                dve.wait_ge(qt_sb, t + 1)
                dve.wait_ge(o_ps, t)
                V.tensor_tensor(qdT[:], BS[0][:].rearrange("p (k t) -> p k t", k=KT), dqT[:],
                                ALU.mult).then_inc(qd_sb, 1)
                normed(t - 1)
                x1t_lo_(0)
                x1t_lo_(1)
                for r in range(QB):
                    dve.wait_ge(score_ps, QB * t + r + 1)
                    V.tensor_tensor(pr[:, r, :], BS[r][:], maskT[:, r, :],
                                    ALU.mult).then_inc(prob_sb, 1)
                    if r == 0:
                        ot_lo_(t - 1)
                x1t_lo_(2)
                x1t_lo_(3)
                add_x1(t - 1)
                gated(t)
                x1t_lo_(4)
                x1t_lo_(5)
                normed(t)

            batches(dve, tile, last_tile)

            def add_y(s, tb):
                dve.wait_ge(y_ps[1], s + 1)
                for j in range(4):
                    row = acc[:, 4 * tb + j, :]
                    V.tensor_tensor(row, row, BY[j][:], ALU.add).then_inc(y_add, 1)

            def step(q, par_q, tb):
                s = TBS * q + tb
                at = s if isinstance(s, int) else None
                dequant = tb >= 1 and not (isinstance(q, int) and q == BLOCKS - 1)
                k = UNITS * (q + 1) + tb - 1
                for par in range(2):
                    dve.wait_ge(h_sq[par], s + 1)
                    V.scalar_tensor_tensor(out=hx[par][:], in0=hx[par][:], scalar=1.0 / GELU_A,
                                           in1=BG[par][:], op0=ALU.add, op1=ALU.mult
                                           ).then_inc(h_arg[par], 1)
                    if par == 0 and dequant:
                        unit_bits(k, tb - 1, [32 * (q + 2) if n == tb - 1 else 0
                                              for n in range(UNITS)])
                    if par == 1 and dequant and at != 1:
                        if tb == 1:
                            dve.wait_ge(y_ps[1], s - 1)
                        unit_scale(k, tb - 1)
                    dve.wait_ge(h_tanh[par], s + 1)
                    V.scalar_tensor_tensor(out=hx[par][:], in0=hx[par][:], scalar=1.0,
                                           in1=BG[par][:], op0=ALU.add, op1=ALU.mult
                                           ).then_inc(h_gelu[par], 1)
                    dve.wait_ge(h_gelu[par], s + 1)
                    dve.wait_ge(u_ps[par], s + 1)
                    V.scalar_tensor_tensor(out=hx[par][:], in0=hx[par][:], scalar=0.5,
                                           in1=BU[par][:], op0=ALU.mult, op1=ALU.mult
                                           ).then_inc(h_prod[par], 1)
                    if par == 0 and not (isinstance(s, int) and s == 0):
                        add_y(s - 1, (tb - 1) % TBS)
                    if at == 0 and par == 0:
                        ot_lo_(TILES - 1)
                    dve.wait_ge(h_hi[par], s + 1)
                    V.tensor_tensor(hl[par][:], hx[par][:], hh[par][:].bitcast(F32),
                                    ALU.subtract).then_inc(h_lo[par], 1)
                    if at == 0 and par == 0:
                        x1t_lo_(6)
                        x1t_lo_(7)
                if at == 0:
                    x1t_lo_(8)
                    x1t_lo_(9)
                    add_x1(TILES - 1)
                    x1t_lo_(10)
                    x1t_lo_(11)
                    stats2(1)
                if at == 1:
                    for t in range(12, TILES):
                        x1t_lo_(t)
                    unit_scale(k, 0)

            pairs(dve, step)
            add_y(TBS * BLOCKS - 1, TBS - 1)

        @block.gpsimd
        def _(pool):
            def rope_b_(t, c):
                pool.wait_ge(qk_silu, t + 1)
                pool.wait_ge(rope_c, t)
                half = "p a (h s d) -> p (a h) s d"
                for s in range(2):
                    ins = nc.gpsimd.tensor_tensor(
                        rb[:].rearrange(half, s=2, d=HD // 2)[:, :, s, :],
                        qa[:].rearrange(half, s=2, d=HD // 2)[:, :, 1 - s, :],
                        rotT[:, 1, c, 16 * s:16 * s + 16].unsqueeze(1)
                        .broadcast_to([P, 2 * HEADS, HD // 2]), ALU.mult)
                ins.then_inc(rope_b, 1)
                pool.wait_ge(rope_a, t + 1)
                pool.wait_ge(rope_b, t + 1)
                nc.gpsimd.tensor_tensor(qr[:], qr[:], rb[:], ALU.add).then_inc(rope_c, 1)

            def decay_k_(b, c, t):
                pool.wait_ge(rope_c, t + 1)
                pool.wait_ge(kv_ps, kvs(b, c))
                nc.gpsimd.tensor_tensor(kd[:].rearrange("p (h d) -> p h d", d=HD),
                                        qr[:, 1, :].rearrange("p (h d) -> p h d", d=HD),
                                        dkT[:].unsqueeze(2).broadcast_to([P, HEADS, HD]),
                                        ALU.mult).then_inc(kd_done, 1)

            def unit_lo(k, u, par):
                pool.wait_ge(dq_hi, k + 1)
                nc.gpsimd.tensor_tensor(
                    wl[par][:, bass.ds(u, 1), :].rearrange("p a w -> p (a w)"),
                    wf[:].rearrange("p a w -> p (a w)"),
                    wh[par][:, bass.ds(u, 1), :].rearrange("p a w -> p (a w)").bitcast(F32),
                    ALU.subtract).then_inc(dq_lo, 1)

            pool.wait_ge(s_whi, 3)
            nc.gpsimd.tensor_tensor(w_lo[2][:], w_in[:, 2, :].rearrange("p (k n) -> p k n", k=KT),
                                    w_hi[2][:].bitcast(F32), ALU.subtract).then_inc(s_vlo, 1)
            pool.wait_ge(s_tab, 16 * 5)
            pool.wait_ge(s_glo, 3)
            rope_b_(0, 0)
            decay_k_(0, 0, 0)

            def tile(b, c):
                t = CHUNKS * b + c
                if c == 3 and not near_end(b, c, 1):
                    unit_lo(b, b, 0)
                if not near_end(b, c, 1):
                    rope_b_(t + 1, (c + 1) % CHUNKS)
                    if c == CHUNKS - 1:
                        decay_k_(b + 1, 0, t + 1)
                    elif c + 1 < CHUNKS - 1:
                        decay_k_(b, c + 1, t + 1)
                if 1 <= c < CHUNKS - 1:
                    pool.wait_ge(inter_ps, kvs(b, c))
                    pool.wait_ge(st_done, kvs(b, c))
                    nc.gpsimd.tensor_tensor(st[:], st[:], lamT[:].unsqueeze(2)
                                            .broadcast_to([P, KT, P]), ALU.mult
                                            ).then_inc(st_scaled, 1)

            def norm2(t):
                if t >= 2:
                    pool.wait_ge(x1t_ps, t - 1)
                pool.wait_ge(s_r2, 1 if t < TILES - CHUNKS else 2)
                nc.gpsimd.tensor_scalar(
                    wf[:, t % 2, :].rearrange("p (j n m) -> p j n m", j=2, n=2),
                    acc[:, t, :].rearrange("p (j m n) -> p j n m", j=2, n=2),
                    r2[:, t:t + 1], nm2[:, t:t + 1], ALU.mult, ALU.add).then_inc(n2_done, 1)

            def last_tile():
                pool.wait_ge(dq_lo, UNITS)
                for t in range(TILES):
                    norm2(t)

            batches(pool, tile, last_tile)

            def step(q, par_q, tb):
                if tb >= 1 and not (isinstance(q, int) and q == BLOCKS - 1):
                    unit_lo(UNITS * (q + 1) + tb - 1, tb - 1, 1 - par_q)

            pairs(pool, step)

        @block.tensor
        def _(pe):
            def split3(dst, ws, xs, start, stop):
                (w_h, w_l), (x_h, x_l) = ws, xs
                pe.matmul(dst, w_h, x_h, start=start, stop=False)
                pe.matmul(dst, w_h, x_l, start=False, stop=False)
                return pe.matmul(dst, w_l, x_h, start=False, stop=stop)

            def project(dst, n):
                for k in range(KT):
                    ins = split3(dst[:], (xth[:, k, :], xtl[:, k, :]),
                                 (w_hi[n][:, k, :], w_lo[n][:, k, :]), k == 0, k == KT - 1)
                return ins

            def transposes(dst, src):
                for k in range(KT):
                    ins = pe.transpose(dst[:, P * k:P * k + P], src[:, P * k:P * k + P], idt[:])
                return ins

            def x_transpose(t):
                pe.wait_ge(xn_done, t + 1)
                pe.wait_ge(v_sb, t)
                transposes(BV, xn).then_inc(xt_ps, 1)

            def qk_transpose(t):
                pe.wait_ge(rope_c, t + 1)
                transposes(BS[0], qr[:, 0, :])
                transposes(BS[1], qr[:, 1, :]).then_inc(qkt_ps, 1)

            def q_ready(t):
                pe.wait_ge(xt_hi, t + 1)
                pe.wait_ge(xt_lo, t + 1)
                pe.wait_ge(qk_silu, t)
                if not (isinstance(t, int) and t < 3):
                    pe.wait_ge(x1_done, t - 2)

            def q_part(k):
                split3(BQ[:], (xth[:, k, :], xtl[:, k, :]), (w_hi[0][:, k, :], w_lo[0][:, k, :]),
                       k == 0, k == KT - 1)

            def k_project(t):
                pe.wait_ge(qk_silu, t)
                if isinstance(t, int) and t == 0:
                    pe.wait_ge(s_wlo, 2)
                project(BK, 1).then_inc(qk_ps, 1)

            def gate1(t):
                pe.wait_ge(gate_tanh, t)
                for k in range(KT):
                    ins = split3(BS[3][:, 0:P], (g1h[:, k, :], g1l[:, k, :]),
                                 (xth[:, k, :], xtl[:, k, :]), k == 0, k == KT - 1)
                ins.then_inc(g1_ps, 1)

            def v_project(t):
                project(BV, 2).then_inc(v_ps, 1)

            def gate2(t):
                pe.wait_ge(g_lo, t + 1)
                pe.wait_ge(prob_sb, QB * t)
                pe.matmul(BS[3][:], g4[:], g2s[:], start=True, stop=True).then_inc(gate_ps, 1)

            def o_transpose(t):
                pe.wait_ge(on_done, t + 1)
                transposes(BO, sq).then_inc(ot_ps, 1)

            def o_ready(t):
                pe.wait_ge(ot_lo, t + 1)
                if not (isinstance(t, int) and t == 0):
                    pe.wait_ge(x1_done, t)

            def o_part(k, dst=BQ):
                ins = split3(dst[:], (oth[:, k, :], otl[:, k, :]),
                             (w_hi[3][:, k, :], w_lo[3][:, k, :]), k == 0, k == KT - 1)
                if k == KT - 1:
                    ins.then_inc(wo_ps, 1)

            def scores(g):
                for r in range(QB):
                    ins = pe.matmul(BS[r][:, P * g:P * g + P], kT[32 * r:32 * r + 32, g, :],
                                    qT[32 * r:32 * r + 32, g, :], start=True, stop=True)
                    if g == KT - 1:
                        ins.then_inc(score_ps, 1)

            def inter():
                for g in range(KT):
                    ins = pe.matmul(BO[:, P * g:P * g + P], qdT[:, g, :], st[:, g, :],
                                    start=(g == 0), stop=False, skip_group_check=True)
                ins.then_inc(inter_ps, 1)

            def intra(t, c, q_between):
                for r in range(QB):
                    pe.wait_ge(prob_sb, QB * t + r + 1)
                    for g in range(KT):
                        h = QB * g + r
                        ins = pe.matmul(BO[:, HD * h:HD * h + HD], pr[:, r, P * g:P * g + P],
                                        vs[:, c % 2, HD * h:HD * h + HD],
                                        start=(c == 0 and r == 0 and g == 0),
                                        stop=(r == QB - 1 and g == KT - 1), skip_group_check=True)
                    if r == QB - 1:
                        ins.then_inc(o_ps, 1)
                    if q_between and r == 0:
                        q_ready(t + 2)
                    if q_between:
                        q_part(r)

            def x1_transpose(t, bank_read):
                pe.wait_ge(n2_done, t + 1)
                if bank_read:
                    pe.wait_ge(x1t_lo, bank_read)
                transposes(BX[t], wf[:, t % 2, :]).then_inc(x1t_ps, 1)

            pe.wait_ge(s_id, 16)
            x_transpose(0)
            pe.wait_ge(s_wlo, 1)
            q_ready(0)
            for k in range(KT):
                q_part(k)
            k_project(0)
            pe.wait_ge(s_glo, 3)
            gate1(0)
            pe.wait_ge(s_vlo, 1)
            v_project(0)
            x_transpose(1)
            gate2(0)
            q_ready(1)
            for k in range(KT):
                q_part(k)

            def tile(b, c):
                t = CHUNKS * b + c
                if not at_start(b, c):
                    qk_transpose(t)
                if not at_start(b, c):
                    pe.wait_ge(st_done, kvs(b, c))
                if not near_end(b, c, 1):
                    k_project(t + 1)
                    if at_start(b, c):
                        qk_transpose(t)
                    gate1(t + 1)
                    v_project(t + 1)
                if not at_start(b, c):
                    o_transpose(t - 1)
                pe.wait_ge(qt_sb, t + 1)
                pe.wait_ge(kt_sb, t + 1)
                pe.wait_ge(qd_sb, t + 1)
                if not near_end(b, c, 1):
                    pe.wait_ge(g_lo, t + 2)
                else:
                    pe.wait_ge(gate_tanh, t + 1)
                scores(0)
                scores(1)
                if not near_end(b, c, 2):
                    x_transpose(t + 2)
                if not near_end(b, c, 1):
                    pe.wait_ge(qk_silu, t + 2)
                if not at_start(b, c):
                    if isinstance(b, int) and b == 0 and c == 1:
                        pe.wait_ge(s_wlo, 3)
                    o_ready(t - 1)
                    o_part(0)
                scores(2)
                if not at_start(b, c):
                    o_part(1)
                scores(3)
                if not at_start(b, c):
                    o_part(2)
                    o_part(3)
                pe.wait_ge(v_sb, t + 1)
                if c < CHUNKS - 1:
                    pe.wait_ge(kd_done, kvs(b, c) + 1)
                    for g in range(KT):
                        ins = pe.matmul(BK[:, P * g:P * g + P], kd[:, P * g:P * g + P],
                                        vs[:, c % 2, P * g:P * g + P], start=True, stop=True)
                    ins.then_inc(kv_ps, 1)
                if c:
                    pe.wait_ge(st_done, kvs(b, c))
                    inter()
                intra(t, c, not near_end(b, c, 2))
                if not near_end(b, c, 1):
                    gate2(t + 1)

            def last_tile():
                t, c = TILES - 1, CHUNKS - 1
                qk_transpose(t)
                pe.wait_ge(st_done, kvs(BATCH - 1, c))
                x1_transpose(0, 0)
                pe.wait_ge(v_sb, t + 1)
                x1_transpose(1, 0)
                pe.wait_ge(kt_sb, t + 1)
                pe.wait_ge(qd_sb, t + 1)
                pe.wait_ge(gate_tanh, t + 1)
                for g in range(KT):
                    scores(g)
                o_transpose(t - 1)
                x1_transpose(2, 1)
                o_ready(t - 1)
                for k in range(KT):
                    o_part(k)
                x1_transpose(3, 2)
                inter()
                intra(t, c, False)

            batches(pe, tile, last_tile)

            def gate_up(q, par_q, tb, par):
                s = TBS * q + tb
                pe.wait_ge(h_prod[par], s)
                for u, dst, done in ((GATE, BG[par], g_ps[par]), (UP, BU[par], u_ps[par])):
                    for k in range(KT):
                        cols = slice(512 * (k % 2) + 256 * (k // 2) + P * par,
                                     512 * (k % 2) + 256 * (k // 2) + P * par + P)
                        ins = split3(dst[:], (wh[par_q][:, u, cols], wl[par_q][:, u, cols]),
                                     (x1h[:, tb, k, :], x1l[:, tb, k, :]), k == 0, k == KT - 1)
                    ins.then_inc(done, 1)

            def down(s, par_q, par):
                pe.wait_ge(h_hi[par], s + 1)
                pe.wait_ge(h_lo[par], s + 1)
                if par == 0:
                    pe.wait_ge(y_add, 4 * s)
                for j in range(4):
                    if isinstance(s, int) and s == 0 and par == 0 and j == 1:
                        pe.wait_ge(x1t_lo, 12)
                    ins = split3(BY[j][:], (hh[par][:, P * j:P * j + P], hl[par][:, P * j:P * j + P]),
                                 (wh[par_q][:, DOWN, 512 * par:512 * par + 512],
                                  wl[par_q][:, DOWN, 512 * par:512 * par + 512]),
                                 par == 0, par == 1)
                ins.then_inc(y_ps[par], 1)

            def step(q, par_q, tb):
                s = TBS * q + tb
                at = s if isinstance(s, int) else None
                if isinstance(q, int) and q == 0:
                    pe.wait_ge(x1t_lo, 4 * (tb + 1))
                if tb == 0:
                    pe.wait_ge(dq_lo, UNITS * (q + 1))
                if at == 0:
                    pe.wait_ge(x1_done, TILES - 1)
                    x1_transpose(4, 4)
                    x1_transpose(5, 4)
                gate_up(q, par_q, tb, 0)
                if at == 0:
                    o_transpose(TILES - 1)
                    x1_transpose(6, 5)
                    x1_transpose(7, 6)
                else:
                    down(s - 1, par_q if tb else 1 - par_q, 1)
                gate_up(q, par_q, tb, 1)
                if at == 0:
                    x1_transpose(8, 7)
                    x1_transpose(9, 8)
                    o_ready(TILES - 1)
                    for k in range(KT):
                        o_part(k, BS[2])
                    x1_transpose(10, 0)
                    x1_transpose(11, 10)
                    pe.wait_ge(x1_done, TILES)
                if at == 1:
                    pe.wait_ge(y_add, 4)
                    for t in range(12, TILES):
                        x1_transpose(t, 0)
                    pe.wait_ge(x1t_lo, TILES)
                down(s, par_q, 0)

            pairs(pe, step)
            down(TBS * BLOCKS - 1, 1, 1)


def pairs(eng, step):
    def pair(n):
        for par_q in range(2):
            for tb in range(TBS):
                step(2 * n + par_q, par_q, tb)

    pair(0)
    with eng.Fori(1, BLOCKS // 2 - 1) as n:
        pair(n)
    pair(BLOCKS // 2 - 1)


def lay_out(inputs):
    def wide(w, last):
        return w.reshape(BLOCKS, P, 2, 2, last).transpose(0, 4, 3, 2, 1).reshape(BLOCKS, last, 512)

    packed = np.stack([wide(inputs["L0_ffn_gate_W_packed"], P), wide(inputs["L0_ffn_up_W_packed"], P),
                       inputs["L0_ffn_down_W_packed"].T.reshape(BLOCKS, P, 512)], axis=1)
    scales = np.stack([wide(inputs["L0_ffn_gate_scales"], 8), wide(inputs["L0_ffn_up_scales"], 8),
                       inputs["L0_ffn_down_scales"].T.reshape(BLOCKS, 8, 512)], axis=1)
    return {
        "x": inputs["L0_attn_x"], "wq": inputs["L0_attn_Wq"], "wk": inputs["L0_attn_Wk"],
        "wv": inputs["L0_attn_Wv"], "wo": inputs["L0_attn_Wo"], "wg1": inputs["L0_attn_Wg1"],
        "wg2": inputs["L0_attn_Wg2"], "norm_w": inputs["L0_attn_norm_weight"].reshape(KT, P).T,
        "packed": packed.reshape(BLOCKS * UNITS, P, 512),
        "scales": scales.reshape(BLOCKS * UNITS, 8, 512),
    } | shape_constants()


def kernel(**inputs):
    import concourse.bacc as bacc
    from concourse.bass_utils import run_bass_kernel_spmd

    arrays = {n: np.ascontiguousarray(a)
              for n, a in lay_out({n: np.asarray(a) for n, a in inputs.items()}).items()}
    nc = bacc.Bacc("TRN2", target_bir_lowering=False, num_devices=1)
    args = {n: nc.dram_tensor(n + "_dram", a.shape, mybir.dt.from_np(a.dtype),
                              kind="ExternalInput").ap() for n, a in arrays.items()}
    out = nc.dram_tensor("out_dram", (BATCH, SEQ, EMBED), F32, kind="ExternalOutput").ap()
    build(nc, out=out, **args)
    r = run_bass_kernel_spmd(nc, [{n + "_dram": a for n, a in arrays.items()}], core_ids=[0])
    return r.results[0]["out_dram"]
```
